# Optimizing a Trainium2 kernel written in Bass

```python
import numpy as np
import jax
import jax.numpy as jnp

def _softmax(x, axis=-1):
    return jax.nn.softmax(x, axis=axis)

def _gelu(x):
    return jax.nn.gelu(x, approximate=True)

def _silu(x):
    return jax.nn.silu(x)

def _sigmoid(x):
    return jax.nn.sigmoid(x)

def _layernorm(x, axis=-1, eps=1e-05):
    m = jnp.mean(x, axis=axis, keepdims=True)
    v = jnp.var(x, axis=axis, keepdims=True)
    return (x - m) / jnp.sqrt(v + eps)

def _scatter_add(tgt, idx, src, axis=0):
    return tgt.at[idx].add(src)

def _segment_sum(src, seg, n):
    return jax.ops.segment_sum(src, seg, n)
kernel_name = 'mk_xattn_ffn_d1_seqx_r4_c1189e'

def setup_inputs(seed: int=0):
    np.random.seed(seed)
    _w = jnp.asarray

    def _rec_inputs():
        import jax
        import jax.numpy as jnp
        _rk = jax.random.key(seed)
        x = -0.0003929 + 0.9999 * jax.random.normal(jax.random.fold_in(_rk, 1), (16, 112, 256), jnp.float32)
        _lenS = 112 - jax.random.randint(jax.random.fold_in(_rk, 7), (16,), 0, max(1, 112 // 4) + 1, jnp.int32)
        _lenS2 = 375 - jax.random.randint(jax.random.fold_in(_rk, 8), (16,), 0, max(1, 375 // 4) + 1, jnp.int32)
        _ctx_1024P = jax.random.normal(jax.random.fold_in(_rk, 11), (16, 16, 256), jnp.float32)
        _ctx_1024c = jax.random.dirichlet(jax.random.fold_in(_rk, 511), 0.3 * jnp.ones((16,), jnp.float32), (16, 375))
        _ctx_1024t = jnp.einsum('bsk,bkd->bsd', _ctx_1024c, _ctx_1024P)
        _ctx_1024t = _ctx_1024t * jax.lax.rsqrt(jnp.mean(jnp.square(_ctx_1024t)) + 1e-12) * 0.953939
        ctx_1024 = 2.81802e-05 + 1.00001 * (_ctx_1024t + 0.3 * jax.random.normal(jax.random.fold_in(_rk, 611), (16, 375, 256), jnp.float32))
        return (x, ctx_1024)
    x, ctx_1024 = _rec_inputs()

    def _L0_xattn_setup():
        import jax, jax.numpy as jnp
        import numpy as np
        DIM = 256
        B, TQ, TK = (8, 512, 512)
        key = jax.random.key(seed)
        ks = jax.random.split(key, 8)
        s = 1.0 / np.sqrt(DIM)
        return {'texto': jax.random.normal(ks[0], (B, TQ, DIM), dtype=jnp.float32), 'imagen': jax.random.normal(ks[1], (B, TK, DIM), dtype=jnp.float32), 'Wq': jax.random.normal(ks[2], (DIM, DIM), dtype=jnp.float32) * s, 'bq': jnp.zeros((DIM,), dtype=jnp.float32), 'Wk': jax.random.normal(ks[3], (DIM, DIM), dtype=jnp.float32) * s, 'bk': jnp.zeros((DIM,), dtype=jnp.float32), 'Wv': jax.random.normal(ks[4], (DIM, DIM), dtype=jnp.float32) * s, 'bv': jnp.zeros((DIM,), dtype=jnp.float32)}
    _L0_xattn_all = _L0_xattn_setup()
    _L0_xattn_in = {k: v for k, v in _L0_xattn_all.items() if k in ('Wq', 'bq', 'Wk', 'bk', 'Wv', 'bv')}
    del _L0_xattn_all

    def _L0_ffn_setup():
        import jax, jax.numpy as jnp
        import numpy as np
        B, S, H = (2, 256, 256)
        E, F = (8, 1024)
        GATE_TEMP = 0.1
        key = jax.random.key(seed)
        ks = jax.random.split(key, 6)
        s_h = 1.0 / np.sqrt(H)
        s_f = 1.0 / np.sqrt(F)
        return {'hidden_states': jax.random.normal(ks[0], (B, S, H), dtype=jnp.float32), 'w_router': jax.random.normal(ks[1], (H, E), dtype=jnp.float32) * s_h, 'w_gating': jax.random.normal(ks[2], (H, E), dtype=jnp.float32) * s_h, 'w_gate': jax.random.normal(ks[3], (E, H, F), dtype=jnp.float32) * s_h, 'w_up': jax.random.normal(ks[4], (E, H, F), dtype=jnp.float32) * s_h, 'w_down': jax.random.normal(ks[5], (E, F, H), dtype=jnp.float32) * s_f}
    _L0_ffn_all = _L0_ffn_setup()
    _L0_ffn_in = {k: v for k, v in _L0_ffn_all.items() if k in ('w_router', 'w_gating', 'w_gate', 'w_up', 'w_down')}
    del _L0_ffn_all
    return {'x': x, 'ctx_1024': ctx_1024, 'L0_xattn_Wq': _L0_xattn_in['Wq'], 'L0_xattn_bq': _L0_xattn_in['bq'], 'L0_xattn_Wk': _L0_xattn_in['Wk'], 'L0_xattn_bk': _L0_xattn_in['bk'], 'L0_xattn_Wv': _L0_xattn_in['Wv'], 'L0_xattn_bv': _L0_xattn_in['bv'], 'L0_ffn_w_router': _L0_ffn_in['w_router'], 'L0_ffn_w_gating': _L0_ffn_in['w_gating'], 'L0_ffn_w_gate': _L0_ffn_in['w_gate'], 'L0_ffn_w_up': _L0_ffn_in['w_up'], 'L0_ffn_w_down': _L0_ffn_in['w_down']}

def reference(x, ctx_1024, L0_xattn_Wq, L0_xattn_bq, L0_xattn_Wk, L0_xattn_bk, L0_xattn_Wv, L0_xattn_bv, L0_ffn_w_router, L0_ffn_w_gating, L0_ffn_w_gate, L0_ffn_w_up, L0_ffn_w_down):
    import jax
    import jax.numpy as jnp

    def _L0_xattn_ref(texto, imagen, Wq, bq, Wk, bk, Wv, bv):
        import jax, jax.numpy as jnp
        import numpy as np
        DIM = 256
        B, TQ, TK = (8, 512, 512)
        q = texto @ Wq + bq
        k = imagen @ Wk + bk
        v = imagen @ Wv + bv
        scale = 1.0 / jnp.sqrt(jnp.asarray(texto.shape[-1], dtype=q.dtype))
        scores = jnp.einsum('bqd,bkd->bqk', q, k) * scale
        attn = jax.nn.softmax(scores, axis=-1)
        return jnp.einsum('bqk,bkd->bqd', attn, v)

    def _L0_ffn_ref(hidden_states, w_router, w_gating, w_gate, w_up, w_down):
        import jax, jax.numpy as jnp
        import numpy as np
        B, S, H = (2, 256, 256)
        E, F = (8, 1024)
        GATE_TEMP = 0.1
        x = hidden_states
        router_probs = jax.nn.softmax(jnp.einsum('bsh,he->bse', x, w_router), axis=-1)
        gate_weights = jax.nn.softmax(jnp.einsum('bsh,he->bse', x, w_gating) / GATE_TEMP, axis=-1)
        g = jnp.einsum('bsh,ehf->ebsf', x, w_gate)
        u = jnp.einsum('bsh,ehf->ebsf', x, w_up)
        h = jax.nn.silu(g) * u
        expert_out = jnp.einsum('ebsf,efh->ebsh', h, w_down)
        cw = router_probs * gate_weights
        cw = cw / (jnp.sum(cw, axis=-1, keepdims=True) + 1e-09)
        out = jnp.einsum('ebsh,bse->bsh', expert_out, cw)
        return out
    x = x + _L0_xattn_ref(_layernorm(x, axis=-1), ctx_1024, L0_xattn_Wq, L0_xattn_bq, L0_xattn_Wk, L0_xattn_bk, L0_xattn_Wv, L0_xattn_bv)
    x = x + _L0_ffn_ref(_layernorm(x, axis=-1), L0_ffn_w_router, L0_ffn_w_gating, L0_ffn_w_gate, L0_ffn_w_up, L0_ffn_w_down)
    return x

_drawn_inputs = setup_inputs


def setup_inputs(seed=0):
    import zlib

    import numpy as np

    out = dict(_drawn_inputs(seed))
    spreads = {'L0_xattn_bq': (0.0, 0.312), 'L0_xattn_bk': (0.0, 0.8), 'L0_xattn_bv': (0.0, 0.1)}
    factors = {}
    for name, (base, spread) in spreads.items():
        noise = np.random.default_rng([zlib.crc32(name.encode()), seed]).standard_normal(out[name].shape)
        drawn = base * np.exp(spread * noise) if base else spread * noise
        out[name] = jnp.asarray(drawn.astype(out[name].dtype))
    for name, factor in factors.items():
        out[name] = (out[name] * factor).astype(out[name].dtype)
    return out
```

```python
import concourse.bass as bass
from concourse import mybir
from contextlib import ExitStack


def xattn_ffn_kernel(nc, x, ctx, wq, bq, wk, bk, wv, bv, w_router, w_gating, w_gate, w_up, w_down, out):
    fp32, fp32r = mybir.dt.float32, mybir.dt.float32r
    ALU, ACT, AX = mybir.AluOpType, mybir.ActivationFunctionType, mybir.AxisListType

    B, TQ, D = x.shape
    TK = ctx.shape[1]
    E, _, F = w_gate.shape
    P = 128
    DK = D // P
    KT = 3
    KP = TK // KT
    SK = TK + TK % 2
    PAIRS = B // 2
    TP = 2 * TQ
    T = B * TQ
    CH = 4
    TC = T // CH
    BC = B // CH
    HALVES = 2
    FH = F // HALVES
    FT = FH // P
    STEPS = HALVES * CH * FT
    LAG = 2
    HS = 4
    SCALE = float(D) ** -0.5
    EPS = 1e-5
    TEMP = 0.1
    DMA = 16

    x_v = x.rearrange("b q d -> q b d")
    out_v = out.rearrange("b q d -> q b d")
    ctx_v = ctx.rearrange("(n two) (p t) d -> n p two (t d)", two=2, t=KT)
    gate_v = w_gate.rearrange("e (k p) (h f) -> e h p k f", p=P, h=HALVES)
    up_v = w_up.rearrange("e (k p) (h f) -> e h p k f", p=P, h=HALVES)
    down_v = w_down.rearrange("e (h t p) d -> e h p t d", p=P, h=HALVES)
    cw_dram = nc.dram_tensor("cw_dram", (E, T), fp32).ap()

    es = ExitStack()
    with es:
        def sb(name, shape, dt=fp32):
            return es.enter_context(nc.sbuf_tensor(name, shape, dt))

        def sem(name):
            return es.enter_context(nc.semaphore(name))

        def at_least(engine, semaphore, count):
            if not isinstance(count, int) or count > 0:
                engine.wait_ge(semaphore, count)

        ident = sb("ident", [P, P])
        ones = sb("ones", [P, TQ])
        eps_c = sb("eps_c", [TQ, 2])
        power_c = sb("power_c", [TQ, 2])
        bq_sb = sb("bq_sb", [P, DK])
        bk_sb = sb("bk_sb", [P, DK])
        bqk_prod = sb("bqk_prod", [P, DK])
        qbias = sb("qbias", [P, DK])
        v_raw = sb("v_raw", [P, DK])
        v_split = sb("v_split", [P, DK, 2], fp32r)
        c0 = sb("c0", [TQ, 1])
        m_hi = sb("m_hi", [P, DK, D], fp32r)
        m_lo = sb("m_lo", [P, DK, D], fp32r)
        wv_hi = sb("wv_hi", [P, DK, D], fp32r)
        wv_lo = sb("wv_lo", [P, DK, D], fp32r)
        wr_raw = sb("wr_raw", [P, DK, 2 * E])
        wr_hi = sb("wr_hi", [P, DK, 2 * E], fp32r)
        wr_lo = sb("wr_lo", [P, DK, 2 * E], fp32r)
        xs = sb("xs", [TQ, B, D])
        h_in_hi = sb("h_in_hi", [P, DK, T], fp32r)
        h_in_lo = sb("h_in_lo", [P, DK, T], fp32r)
        w_raw = sb("w_raw", [P, 3, DK * FH])
        w_hi = sb("w_hi", [P, HALVES, 3, DK * FH], fp32r)
        w_lo = sb("w_lo", [P, HALVES, 3, DK * FH], fp32r)
        cn_hi = sb("cn_hi", [KP, 2, KT, D], fp32r)
        cn_lo = sb("cn_lo", [KP, 2, KT, D], fp32r)
        ct_hi = sb("ct_hi", [P, 2, DK, SK], fp32r)
        ct_lo = sb("ct_lo", [P, 2, DK, SK], fp32r)
        xt_hi = sb("xt_hi", [P, DK, TP], fp32r)
        xt_lo = sb("xt_lo", [P, DK, TP], fp32r)
        q_hi = sb("q_hi", [P, DK, TP], fp32r)
        q_lo = sb("q_lo", [P, DK, TP], fp32r)
        pt_hi = sb("pt_hi", [KP, 2, KT, TQ], fp32r)
        pt_lo = sb("pt_lo", [KP, 2, KT, TQ], fp32r)
        st_hi = sb("st_hi", [P, DK, TP], fp32r)
        st_lo = sb("st_lo", [P, DK, TP], fp32r)
        bn1 = sb("bn1", [TQ, 2, 6])
        mv1 = sb("mv1", [TQ, 2, 2])
        var1 = sb("var1", [TQ, 2])
        rstd1 = sb("rstd1", [TQ, 2])
        bn2 = sb("bn2", [TQ, 2, 6])
        mv2 = sb("mv2", [TQ, 2, 2])
        var2 = sb("var2", [TQ, 2])
        rstd2 = sb("rstd2", [TQ, 2])
        q_bk = sb("q_bk", [TQ, 2])
        top = sb("top", [TQ, 2])
        top_all = sb("top_all", [TQ, 2])
        neg_top = sb("neg_top", [TQ, 2])
        mass = sb("mass", [TQ, 2])
        inv_mass = sb("inv_mass", [TQ, 2])
        logits = sb("logits", [TQ, B, 2 * E])
        lg = sb("lg", [TQ, B * 2, E])
        lg_top = sb("lg_top", [TQ, B * 2])
        lg_sum = sb("lg_sum", [TQ, B * 2])
        cw = sb("cw", [TQ, B, E])
        cw_sum = sb("cw_sum", [TQ, B])
        cw_t = sb("cw_t", [TQ, E, B])
        cw_rows = sb("cw_rows", [P, TQ])
        cw_all = sb("cw_all", [P, T])
        acc = sb("acc", [P, DK, T])
        acc_f = acc[:, :, :].rearrange("p k t -> p (k t)")
        ctx_raw = acc_f[0:KP, 0:2 * KT * D].rearrange("p (b n) -> p b n", b=2)
        at0 = 2 * KT * D
        xn = acc_f[0:TQ, at0:at0 + 2 * D].rearrange("p (b n) -> p b n", b=2)
        at0 += 2 * D
        probs = acc_f[0:TQ, at0:at0 + 2 * TK].rearrange("p (b n) -> p b n", b=2)
        at0 += 2 * TK
        mix = acc_f[0:TQ, at0:at0 + 2 * D].rearrange("p (b n) -> p b n", b=2)
        part = sb("part", [P, 2, DK, TC])
        part_f = part[:, :, :, :].rearrange("p s k t -> p (s k t)")
        xn2 = part_f[0:TQ, 0:2 * D].rearrange("p (b n) -> p b n", b=2)
        bv_all = part_f[0:TQ, 2 * D:3 * D]
        hs = sb("hs", [P, 2, HS, TC], fp32r)
        hs_f = hs[:, :, :, :].rearrange("p a s t -> p (a s t)")
        wt = [hs_f[:, i * DK * D:(i + 1) * DK * D].rearrange("p (k n) -> p k n", k=DK) for i in range(4)]
        wqt_hi, wqt_lo, wkt_hi, wkt_lo = wt
        at0 = 4 * DK * D
        at_hi, at_lo = [hs_f[:, at0 + i * DK * TP:at0 + (i + 1) * DK * TP].rearrange("p (k n) -> p k n", k=DK)
                        for i in range(2)]
        wqk_raw = [w_raw[:, 0, i * DK * D:(i + 1) * DK * D].rearrange("p (k n) -> p k n", k=DK) for i in range(2)]
        wv_raw = w_raw[:, 1, 0:DK * D].rearrange("p (k n) -> p k n", k=DK)
        act = sb("act", [P, 2, TC])
        hid = sb("hid", [P, 2, TC])

        ps = es.enter_context(nc.psum_tensor("ps", [P, 8, 512], fp32))
        ps_x = ps[:, 0, 0:DK * TP].rearrange("p (k t) -> p k t", k=DK)
        ps_qb = ps[0:TQ, 0, DK * TP:DK * TP + 4].rearrange("p (b n) -> p b n", b=2)
        ps_c = ps[:, 1:3, 0:TK]
        ps_s = [ps[0:TQ, 3 + b, 0:SK] for b in range(2)]
        ps_p = [ps[0:KP, 3 + b, 0:KT * TQ].rearrange("p (t q) -> p t q", t=KT) for b in range(2)]
        ps_a = ps[0:TQ, 5, :].rearrange("p (b n) -> p b n", b=2)
        ps_at = ps[:, 5, 0:DK * TP].rearrange("p (k t) -> p k t", k=DK)
        ps_o = ps[0:TQ, 6, :].rearrange("p (b n) -> p b n", b=2)
        ps_x2 = ps[:, 7, 0:DK * TP].rearrange("p (k t) -> p k t", k=DK)
        ps_l = ps[0:TQ, 7, DK * TP:DK * TP + 4 * E].rearrange("p (b n) -> p b n", b=2)
        ps_wt = [ps[:, 1 + i, :].rearrange("p (k n) -> p k n", k=DK) for i in range(2)]
        ps_m = ps[:, 3, :].rearrange("p (k n) -> p k n", k=DK)
        ps_b = ps[:, 4, 0:8]
        ps_g = [ps[:, i, 0:TC] for i in range(2)]
        ps_u = [ps[:, 2 + i, 0:TC] for i in range(2)]
        ps_d = [ps[:, 4 + 2 * i:6 + 2 * i, 0:TC] for i in range(2)]
        ps_cw = ps[:, 6, 0:TQ]

        x_first, x_rest = sem("x_first"), sem("x_rest")
        weights_in, biases_in, router_in = sem("weights_in"), sem("biases_in"), sem("router_in")
        zeros_set, consts_set = sem("zeros_set"), sem("consts_set")
        wt_ready, wt_hi_done, wt_lo_done = sem("wt_ready"), sem("wt_hi_done"), sem("wt_lo_done")
        m_ready, m_hi_done, m_lo_done = sem("m_ready"), sem("m_hi_done"), sem("m_lo_done")
        prod_done, vb_ready, vb_raw, vb_hi, vb_done = (sem(n) for n in ("prod_done", "vb_ready", "vb_raw", "vb_hi", "vb_done"))
        wv_hi_done, wv_lo_done = sem("wv_hi_done"), sem("wv_lo_done")
        xt_ready, ct_ready, q_ready = sem("xt_ready"), sem("ct_ready"), sem("q_ready")
        scores_ready, pt_ready, mix_ready = sem("scores_ready"), sem("pt_ready"), sem("mix_ready")
        at_ready, o_ready, x2t_ready, logits_ready = sem("at_ready"), sem("o_ready"), sem("x2t_ready"), sem("logits_ready")
        xt_hi_done, ct_hi_done, q_hi_done, probs_done = sem("xt_hi_done"), sem("ct_hi_done"), sem("q_hi_done"), sem("probs_done")
        pt_hi_done, mix_done, at_hi_done, st_hi_done = sem("pt_hi_done"), sem("mix_done"), sem("at_hi_done"), sem("st_hi_done")
        xt_lo_done, ct_lo_done, q_lo_done, pt_lo_done = sem("xt_lo_done"), sem("ct_lo_done"), sem("q_lo_done"), sem("pt_lo_done")
        at_lo_done, st_lo_done = sem("at_lo_done"), sem("st_lo_done")
        stats1_done, xn_done = sem("stats1_done"), sem("xn_done")
        stats2_done, xn2_done = sem("stats2_done"), sem("xn2_done")
        top_done, top_all_done, neg_top_done, mass_inverted = sem("top_done"), sem("top_all_done"), sem("neg_top_done"), sem("mass_inverted")
        x1_done, logits_done = sem("x1_done"), sem("logits_done")
        var1_done, rstd1_done, var2_done, rstd2_done = sem("var1_done"), sem("rstd1_done"), sem("var2_done"), sem("rstd2_done")
        bv_added, cn_hi_done, cn_lo_done = sem("bv_added"), sem("cn_hi_done"), sem("cn_lo_done")
        ctx_in, h_in_done = sem("ctx_in"), sem("h_in_done")
        cw_step, lg_exp, cw_ready, cw_rows_ready, cw_rows_done, cw_stored = (
            sem(n) for n in ("cw_step", "lg_exp", "cw_ready", "cw_rows_ready", "cw_rows_done", "cw_stored"))
        cw_in = [sem(f"cw_in{c}") for c in range(CH)]
        w_in, w_hi_done, w_done = sem("w_in"), sem("w_hi_done"), sem("w_done")
        gate_ready, up_ready, down_ready = sem("gate_ready"), sem("up_ready"), sem("down_ready")
        act_done, hid_done, hid_hi_done, hid_lo_done = sem("act_done"), sem("hid_done"), sem("hid_hi_done"), sem("hid_lo_done")
        part_done, acc_done = sem("part_done"), sem("acc_done")
        y_ready, y_done, stored = sem("y_ready"), sem("y_done"), sem("stored")

        def three(w_high, w_low, m_high, m_low):
            return [(w_high, m_high), (w_high, m_low), (w_low, m_high)]

        def accumulate(dst, passes, first=True, last=True):
            for i, (w, m) in enumerate(passes):
                ins = nc.tensor.matmul(dst, w, m, start=first and i == 0, stop=last and i == len(passes) - 1)
            return ins

        def low(dst, src, high):
            return nc.vector.tensor_tensor(dst, src, high.bitcast(fp32), ALU.subtract)

        def half_weights(parts, half):
            gate = parts[:, half, 0, :].rearrange("p (k f) -> p k f", k=DK)
            up = parts[:, half, 1, :].rearrange("p (k f) -> p k f", k=DK)
            down = parts[:, half, 2, :].rearrange("p (t d) -> p t d", t=FT)
            return gate, up, down

        pieces = [(i, slice(j * 512, (j + 1) * 512)) for i in range(3) for j in range(DK * FH // 512)]

        block = es.enter_context(nc.Block())

        @block.sync
        def _(sp):
            sp.dma_start(xs[:, 0:2, :], x_v[:, 0:2, :]).then_inc(x_first, DMA)
            sp.dma_start(ctx_raw, ctx_v[0]).then_inc(ctx_in, DMA)
            for src, dst in ((wq, wqk_raw[0]), (wk, wqk_raw[1]), (wv, wv_raw)):
                sp.dma_start(dst, src.rearrange("(k p) n -> p k n", p=P)).then_inc(weights_in, DMA)
            with nc.allow_non_contiguous_dma("a few short rows"):
                for src, dst in ((bq, bq_sb), (bk, bk_sb)):
                    sp.dma_start(dst[:], src.rearrange("(k p) -> p k", p=P)).then_inc(biases_in, DMA)
                sp.dma_start(bv_all, bv[None, :].broadcast_to((TQ, D))).then_inc(biases_in, DMA)
                sp.dma_start(wr_raw[:, :, 0:E], w_router.rearrange("(k p) n -> p k n", p=P)).then_inc(router_in, DMA)
                sp.dma_start(wr_raw[:, :, E:2 * E], w_gating.rearrange("(k p) n -> p k n", p=P)).then_inc(router_in, DMA)
            sp.dma_start(xs[:, 2:B, :], x_v[:, 2:B, :]).then_inc(x_rest, DMA)

            def load_ctx(p):
                sp.wait_ge(ct_ready, 2 * p)
                sp.wait_ge(cn_lo_done, 2 * p)
                sp.dma_start(ctx_raw, ctx_v[p]).then_inc(ctx_in, DMA)

            def keep_input(p):
                sp.wait_ge(st_hi_done, p + 1)
                sp.wait_ge(st_lo_done, p + 1)
                sp.dma_start(h_in_hi[:, :, bass.ds(p * TP, TP)].bitcast(fp32), st_hi[:, :, :].bitcast(fp32)).then_inc(h_in_done, DMA)
                sp.dma_start(h_in_lo[:, :, bass.ds(p * TP, TP)].bitcast(fp32), st_lo[:, :, :].bitcast(fp32)).then_inc(h_in_done, DMA)

            def load_weights(e, half):
                at_least(sp, w_done, 2 * e + half)
                for i, v in enumerate((gate_v, up_v)):
                    sp.dma_start(w_raw[:, i, :].rearrange("p (k f) -> p k f", k=DK), v[e, half]).then_inc(w_in, DMA)
                sp.dma_start(w_raw[:, 2, :].rearrange("p (t d) -> p t d", t=FT), down_v[e, half]).then_inc(w_in, DMA)

            def load_cw(e, c):
                sp.dma_start(cw_all[:, c * TC:(c + 1) * TC],
                             cw_dram[e, c * TC:(c + 1) * TC][None, :].broadcast_to((P, TC))).then_inc(cw_in[c], DMA)

            load_ctx(1)
            sp.wait_ge(wt_ready, 2)
            sp.wait_ge(wv_lo_done, 1)
            load_weights(0, 0)
            load_ctx(2)
            with sp.Fori(1, PAIRS - 2) as p:
                keep_input(p - 1)
                load_ctx(p + 2)
            load_weights(0, 1)
            for p in range(PAIRS - 3, PAIRS):
                keep_input(p)
            sp.wait_ge(cw_rows_done, 1)
            sp.dma_start(cw_dram.rearrange("e (b t) -> (e b) t", t=TQ), cw_rows[:, :]).then_inc(cw_stored, DMA)
            sp.wait_ge(cw_stored, DMA)
            for c in range(CH):
                load_cw(0, c)
            with sp.Fori(0, E - 1) as e:
                load_weights(e + 1, 0)
                load_weights(e + 1, 1)
                for c in range(CH):
                    sp.wait_ge(part_done, 2 * CH * e + CH + c + 1)
                    load_cw(e + 1, c)
            for b in range(B):
                sp.wait_ge(y_done, b + 1)
                sp.dma_start(out_v[:, b, :], xs[:, b, :]).then_inc(stored, DMA)
            sp.wait_ge(stored, DMA * B)

        @block.gpsimd
        def _(pool):
            nc.gpsimd.memset(ident[:], 0.0).then_inc(zeros_set, 1)
            nc.gpsimd.memset(eps_c[:], EPS)
            nc.gpsimd.memset(power_c[:], -0.5)
            nc.gpsimd.memset(ones[:], 1.0)
            if SK > TK:
                for t in (ct_hi, ct_lo):
                    nc.gpsimd.memset(t[:, :, :, TK:SK].bitcast(fp32), 0.0)
            pool.wait_ge(zeros_set, 1)
            nc.gpsimd.affine_select(out=ident[:], in_=ident[:], compare_op=ALU.not_equal, fill=1.0, base=0,
                                    pattern=[[-1, P]], channel_multiplier=1).then_inc(consts_set, 1)
            pool.wait_ge(consts_set, 1)

            def reciprocal_root(mv, var, root, p, ready, var_sem, done):
                pool.wait_ge(ready, p + 1)
                nc.gpsimd.tensor_tensor(var[:], mv[:, :, 1], eps_c[:], ALU.add).then_inc(var_sem, 1)
                pool.wait_ge(var_sem, p + 1)
                nc.gpsimd.tensor_tensor(root[:], var[:], power_c[:], ALU.pow).then_inc(done, 1)

            def low_ctx(p):
                for b in range(2):
                    pool.wait_ge(cn_hi_done, 2 * p + b + 1)
                    nc.gpsimd.tensor_tensor(cn_lo[:, b, :, :], ctx_raw[:, b, :].rearrange("p (t d) -> p t d", t=KT),
                                            cn_hi[:, b, :, :].bitcast(fp32), ALU.subtract).then_inc(cn_lo_done, 1)

            def add_bv(p):
                pool.wait_ge(xn_done, p + 1)
                for b in range(2):
                    rows = xs[:, bass.ds(2 * p + b, 1), :]
                    ins = nc.gpsimd.tensor_tensor(rows, rows, bv_all[:, None, :], ALU.add)
                ins.then_inc(bv_added, 1)

            def low_weights(e, half):
                n = 2 * e + half
                pool.wait_ge(w_hi_done, n + 1)
                for i, s in pieces:
                    ins = nc.gpsimd.tensor_tensor(w_lo[:, half, i, s], w_raw[:, i, s], w_hi[:, half, i, s].bitcast(fp32), ALU.subtract)
                ins.then_inc(w_done, 1)

            reciprocal_root(mv1, var1, rstd1, 0, stats1_done, var1_done, rstd1_done)
            low_ctx(0)
            pool.wait_ge(biases_in, 3 * DMA)
            add_bv(0)

            def pair(p):
                reciprocal_root(mv1, var1, rstd1, p + 1, stats1_done, var1_done, rstd1_done)
                add_bv(p + 1)
                low_ctx(p + 1)
                reciprocal_root(mv2, var2, rstd2, p, stats2_done, var2_done, rstd2_done)

            pair(0)
            low_weights(0, 0)
            with pool.Fori(1, PAIRS - 1) as p:
                pair(p)
            low_weights(0, 1)
            reciprocal_root(mv2, var2, rstd2, PAIRS - 1, stats2_done, var2_done, rstd2_done)

            def add_part(k, c):
                pool.wait_ge(part_done, k + 1)
                at_least(pool, acc_done, k - 2 * CH + 1)
                a = acc[:, :, c * TC:(c + 1) * TC]
                nc.gpsimd.tensor_tensor(a, a, part[:, c % 2, :, :], ALU.add).then_inc(acc_done, 1)

            def expert(e, first=False, last=False):
                if not first:
                    add_part(2 * CH * e - 1, CH - 1)
                    low_weights(e, 1)
                    for c in range(CH):
                        add_part(2 * CH * e + c, c)
                if not last:
                    low_weights(e + 1, 0)
                for c in range(CH if last else CH - 1):
                    add_part(2 * CH * e + CH + c, c)

            expert(0, first=True)
            with pool.Fori(1, E - 1) as e:
                expert(e)
            expert(E - 1, last=True)

        @block.scalar
        def _(sc):
            for i, hi in enumerate((wqt_hi, wkt_hi)):
                sc.wait_ge(wt_ready, i + 1)
                nc.scalar.copy(hi, ps_wt[i]).then_inc(wt_hi_done, 1)
            sc.wait_ge(weights_in, 3 * DMA)
            nc.scalar.copy(wv_hi[:], wv_raw).then_inc(wv_hi_done, 1)
            sc.wait_ge(router_in, 2 * DMA)
            nc.scalar.copy(wr_hi[:], wr_raw[:]).then_inc(wv_hi_done, 1)
            sc.wait_ge(m_ready, 1)
            nc.scalar.mul(m_hi[:], ps_m, SCALE).then_inc(m_hi_done, 1)

            def xt_high(p):
                sc.wait_ge(xt_ready, p + 1)
                nc.scalar.copy(xt_hi[:], ps_x).then_inc(xt_hi_done, 1)

            def ct_high(p, b):
                sc.wait_ge(ct_ready, 2 * p + b + 1)
                nc.scalar.copy(ct_hi[:, b, :, 0:TK], ps_c).then_inc(ct_hi_done, 1)

            def q_high(p):
                sc.wait_ge(q_ready, p + 1)
                for j in range(DK):
                    ins = nc.scalar.activation(q_hi[:, j, :], ps_x[:, j, :], ACT.Identity, bias=qbias[:, j:j + 1])
                ins.then_inc(q_hi_done, 1)

            def exponentials(p):
                sc.wait_ge(neg_top_done, p + 1)
                for b in range(2):
                    nc.scalar.activation(probs[:, b, :], ps_s[b][:, 0:TK], ACT.Exp, bias=neg_top[:, b:b + 1],
                                         accum_out=mass[:, b:b + 1]).then_inc(probs_done, 1)

            def pt_high(p, b):
                sc.wait_ge(pt_ready, 2 * p + b + 1)
                nc.scalar.copy(pt_hi[:, b, :, :], ps_p[b]).then_inc(pt_hi_done, 1)

            def normalise(p):
                sc.wait_ge(mix_ready, p + 1)
                sc.wait_ge(mass_inverted, p + 1)
                for b in range(2):
                    ins = nc.scalar.activation(mix[:, b, :], ps_a[:, b, :], ACT.Identity, scale=inv_mass[:, b:b + 1])
                ins.then_inc(mix_done, 1)

            def at_high(p):
                sc.wait_ge(at_ready, p + 1)
                nc.scalar.copy(at_hi, ps_at).then_inc(at_hi_done, 1)

            def st_high(p):
                sc.wait_ge(x2t_ready, p + 1)
                at_least(sc, h_in_done, 2 * DMA * p)
                nc.scalar.copy(st_hi[:], ps_x2).then_inc(st_hi_done, 1)

            def cn_high(p):
                sc.wait_ge(ctx_in, DMA * (p + 1))
                at_least(sc, mix_ready, p)
                for b in range(2):
                    nc.scalar.copy(cn_hi[:, b, :, :], ctx_raw[:, b, :].rearrange("p (t d) -> p t d", t=KT)).then_inc(cn_hi_done, 1)

            def high_weights(e, half):
                n = 2 * e + half
                sc.wait_ge(w_in, 3 * DMA * (n + 1))
                at_least(sc, down_ready, CH * (n - 1))
                for i, s in pieces:
                    ins = nc.scalar.copy(w_hi[:, half, i, s], w_raw[:, i, s])
                ins.then_inc(w_hi_done, 1)

            cn_high(0)
            xt_high(0)
            ct_high(0, 0)
            ct_high(0, 1)
            sc.wait_ge(vb_done, 1)
            q_high(0)

            def pair(p, first=False, last=False):
                exponentials(p)
                if not last:
                    xt_high(p + 1)
                    ct_high(p + 1, 0)
                pt_high(p, 0)
                pt_high(p, 1)
                if not last:
                    ct_high(p + 1, 1)
                normalise(p)
                if not last:
                    cn_high(p + 1)
                    q_high(p + 1)
                at_high(p)
                if not first:
                    st_high(p - 1)

            pair(0, first=True)
            high_weights(0, 0)
            with sc.Fori(1, PAIRS - 1) as p:
                pair(p)
            high_weights(0, 1)
            pair(PAIRS - 1, last=True)
            st_high(PAIRS - 1)

            sc.wait_ge(cw_step, 2)
            lgv = lg[:, :, :].rearrange("p (b two) e -> p b two e", two=2)
            nc.scalar.activation(lgv[:, :, 0, :], lgv[:, :, 0, :], ACT.Exp)
            nc.scalar.activation(lgv[:, :, 1, :], lgv[:, :, 1, :], ACT.Exp, scale=1.0 / TEMP).then_inc(lg_exp, 1)

            def expert(e, first=False, last=False):
                for s in range(STEPS):
                    n = STEPS * e + s
                    if s == LAG and not first:
                        high_weights(e, 1)
                    if s == STEPS // 2 + LAG and not last:
                        high_weights(e + 1, 0)
                    sc.wait_ge(gate_ready, n + 1)
                    at_least(sc, hid_done, n - 1)
                    nc.scalar.activation(act[:, s % 2, :], ps_g[s % 2], ACT.Silu).then_inc(act_done, 1)
                    sc.wait_ge(hid_done, n + 1)
                    nc.scalar.copy(hs[:, 0, s % HS, :], hid[:, s % 2, :]).then_inc(hid_hi_done, 1)

            expert(0, first=True)
            with sc.Fori(1, E - 1) as e:
                expert(e)
            expert(E - 1, last=True)

        @block.vector
        def _(ve):
            def stats1(p):
                for b in range(2):
                    ins = nc.vector.bn_stats(bn1[:, b, :], xs[:, bass.ds(2 * p + b, 1), :])
                nc.vector.drain()
                for b in range(2):
                    ins = nc.vector.bn_aggr(mv1[:, b, :], bn1[:, b, :])
                ins.then_inc(stats1_done, 1)

            def norm1(p):
                ve.wait_ge(rstd1_done, p + 1)
                for b in range(2):
                    ins = nc.vector.tensor_scalar(xn[:, b, :], xs[:, bass.ds(2 * p + b, 1), :], mv1[:, b, 0:1], rstd1[:, b:b + 1],
                                                  ALU.subtract, ALU.mult)
                ins.then_inc(xn_done, 1)

            def xt_low(p):
                ve.wait_ge(xt_hi_done, p + 1)
                low(xt_lo[:], ps_x, xt_hi[:]).then_inc(xt_lo_done, 1)

            def ct_low(p, b):
                ve.wait_ge(ct_hi_done, 2 * p + b + 1)
                low(ct_lo[:, b, :, 0:TK], ps_c, ct_hi[:, b, :, 0:TK]).then_inc(ct_lo_done, 1)

            def q_low(p):
                ve.wait_ge(q_hi_done, p + 1)
                nc.vector.tensor_reduce(q_bk[:], ps_qb, AX.X, ALU.add)
                for j in range(DK):
                    ins = nc.vector.scalar_tensor_tensor(q_lo[:, j, :], ps_x[:, j, :], qbias[:, j:j + 1],
                                                         q_hi[:, j, :].bitcast(fp32), ALU.add, ALU.subtract)
                ins.then_inc(q_lo_done, 1)

            def maxima(p):
                for b in range(2):
                    ve.wait_ge(scores_ready, 2 * p + b + 1)
                    ins = nc.vector.tensor_reduce(top[:, b:b + 1], ps_s[b][:, 0:TK], AX.X, ALU.max)
                ins.then_inc(top_done, 1)
                ve.wait_ge(top_done, p + 1)
                nc.vector.scalar_tensor_tensor(top_all[:], q_bk[:], c0[:, 0:1], top[:], ALU.add, ALU.add).then_inc(top_all_done, 1)
                ve.wait_ge(top_all_done, p + 1)
                nc.vector.scalar_tensor_tensor(neg_top[:], q_bk[:], c0[:, 0:1], top_all[:], ALU.add, ALU.subtract).then_inc(neg_top_done, 1)

            def pt_low(p, b):
                ve.wait_ge(pt_hi_done, 2 * p + b + 1)
                low(pt_lo[:, b, :, :], ps_p[b], pt_hi[:, b, :, :]).then_inc(pt_lo_done, 1)

            def invert_mass(p):
                ve.wait_ge(probs_done, 2 * p + 2)
                nc.vector.reciprocal(inv_mass[:], mass[:]).then_inc(mass_inverted, 1)

            def at_low(p):
                ve.wait_ge(at_hi_done, p + 1)
                low(at_lo, ps_at, at_hi).then_inc(at_lo_done, 1)

            def st_low(p):
                ve.wait_ge(st_hi_done, p + 1)
                low(st_lo[:], ps_x2, st_hi[:]).then_inc(st_lo_done, 1)

            def residual1(p):
                ve.wait_ge(o_ready, p + 1)
                ve.wait_ge(bv_added, p + 1)
                rows = xs[:, bass.ds(2 * p, 2), :]
                nc.vector.tensor_tensor(rows, rows, ps_o, ALU.add).then_inc(x1_done, 1)
                nc.vector.drain()
                for b in range(2):
                    ins = nc.vector.bn_stats(bn2[:, b, :], xs[:, bass.ds(2 * p + b, 1), :])
                nc.vector.drain()
                for b in range(2):
                    ins = nc.vector.bn_aggr(mv2[:, b, :], bn2[:, b, :])
                ins.then_inc(stats2_done, 1)

            def norm2(p):
                ve.wait_ge(rstd2_done, p + 1)
                for b in range(2):
                    ins = nc.vector.tensor_scalar(xn2[:, b, :], xs[:, bass.ds(2 * p + b, 1), :], mv2[:, b, 0:1], rstd2[:, b:b + 1],
                                                  ALU.subtract, ALU.mult)
                ins.then_inc(xn2_done, 1)

            def keep_logits(p):
                ve.wait_ge(logits_ready, p + 1)
                nc.vector.tensor_copy(logits[:, bass.ds(2 * p, 2), :], ps_l).then_inc(logits_done, 1)

            ve.wait_ge(x_first, DMA)
            stats1(0)
            ve.wait_ge(biases_in, 3 * DMA)
            nc.vector.tensor_tensor(bqk_prod[:], bq_sb[:], bk_sb[:], ALU.mult).then_inc(prod_done, 1)
            norm1(0)
            for i, (hi, lo) in enumerate(((wqt_hi, wqt_lo), (wkt_hi, wkt_lo))):
                ve.wait_ge(wt_hi_done, i + 1)
                low(lo, ps_wt[i], hi).then_inc(wt_lo_done, 1)
            ve.wait_ge(wv_hi_done, 2)
            low(wv_lo[:], wv_raw, wv_hi[:]).then_inc(wv_lo_done, 1)
            low(wr_lo[:], wr_raw[:], wr_hi[:]).then_inc(wv_lo_done, 1)
            ve.wait_ge(m_hi_done, 1)
            nc.vector.scalar_tensor_tensor(m_lo[:], ps_m, SCALE, m_hi[:].bitcast(fp32), ALU.mult, ALU.subtract).then_inc(m_lo_done, 1)
            ve.wait_ge(vb_ready, 1)
            nc.vector.tensor_scalar(qbias[:], ps_b[:, 0:DK], SCALE, None, ALU.mult)
            nc.vector.tensor_scalar(c0[:], ps_b[0:TQ, 2 * DK:2 * DK + 1], SCALE, None, ALU.mult)
            nc.vector.tensor_scalar(v_raw[:], ps_b[:, DK:2 * DK], SCALE, None, ALU.mult).then_inc(vb_raw, 1)
            ve.wait_ge(vb_raw, 1)
            nc.vector.tensor_copy(v_split[:, :, 0], v_raw[:]).then_inc(vb_hi, 1)
            ve.wait_ge(vb_hi, 1)
            low(v_split[:, :, 1], v_raw[:], v_split[:, :, 0]).then_inc(vb_done, 1)
            xt_low(0)
            ct_low(0, 0)
            ct_low(0, 1)
            q_low(0)
            ve.wait_ge(x_rest, DMA)

            def pair(p, first=False, last=False):
                if not last:
                    stats1(p + 1)
                if not first:
                    norm2(p - 1)
                ve.wait_ge(q_lo_done, p + 1)
                maxima(p)
                if not last:
                    norm1(p + 1)
                    xt_low(p + 1)
                    ct_low(p + 1, 0)
                pt_low(p, 0)
                pt_low(p, 1)
                if not last:
                    ct_low(p + 1, 1)
                invert_mass(p)
                if not last:
                    q_low(p + 1)
                at_low(p)
                if not first:
                    st_low(p - 1)
                residual1(p)
                if not first:
                    keep_logits(p - 1)

            pair(0, first=True)
            with ve.Fori(1, PAIRS - 1) as p:
                pair(p)
            pair(PAIRS - 1, last=True)
            norm2(PAIRS - 1)
            st_low(PAIRS - 1)
            keep_logits(PAIRS - 1)

            lv = logits[:, :, :].rearrange("p b (two e) -> p (b two) e", two=2)
            ve.wait_ge(logits_done, PAIRS)
            nc.vector.tensor_reduce(lg_top[:], lv, AX.X, ALU.max).then_inc(cw_step, 1)
            ve.wait_ge(cw_step, 1)
            nc.vector.tensor_tensor(lg[:], lv, lg_top[:, :, None].broadcast_to((TQ, 2 * B, E)), ALU.subtract).then_inc(cw_step, 1)
            ve.wait_ge(lg_exp, 1)
            nc.vector.tensor_reduce(lg_sum[:], lg[:], AX.X, ALU.add).then_inc(cw_step, 1)
            ve.wait_ge(cw_step, 3)
            nc.vector.reciprocal(lg_top[:], lg_sum[:]).then_inc(cw_step, 1)
            ve.wait_ge(cw_step, 4)
            nc.vector.tensor_tensor(lg[:], lg[:], lg_top[:, :, None].broadcast_to((TQ, 2 * B, E)), ALU.mult).then_inc(cw_step, 1)
            ve.wait_ge(cw_step, 5)
            lgv = lg[:, :, :].rearrange("p (b two) e -> p b two e", two=2)
            nc.vector.tensor_tensor(cw[:], lgv[:, :, 0, :], lgv[:, :, 1, :], ALU.mult).then_inc(cw_step, 1)
            ve.wait_ge(cw_step, 6)
            nc.vector.tensor_reduce(cw_sum[:], cw[:], AX.X, ALU.add).then_inc(cw_step, 1)
            ve.wait_ge(cw_step, 7)
            nc.vector.tensor_scalar(cw_sum[:], cw_sum[:], 1e-9, None, ALU.add).then_inc(cw_step, 1)
            ve.wait_ge(cw_step, 8)
            nc.vector.reciprocal(lg_sum[:, 0:B], cw_sum[:]).then_inc(cw_step, 1)
            ve.wait_ge(cw_step, 9)
            nc.vector.tensor_tensor(cw_t[:, :, :].rearrange("p e b -> p b e"), cw[:],
                                    lg_sum[:, 0:B, None].broadcast_to((TQ, B, E)), ALU.mult).then_inc(cw_ready, 1)

            def expert(e, first=False, last=False):
                for s in range(STEPS + (LAG if last else 0)):
                    n = STEPS * e + s
                    if s < STEPS:
                        ve.wait_ge(act_done, n + 1)
                        ve.wait_ge(up_ready, n + 1)
                        at_least(ve, hid_hi_done, n - 1)
                        nc.vector.tensor_tensor(hid[:, s % 2, :], act[:, s % 2, :], ps_u[s % 2], ALU.mult).then_inc(hid_done, 1)
                        ve.wait_ge(hid_hi_done, n + 1)
                        low(hs[:, 1, s % HS, :], hid[:, s % 2, :], hs[:, 0, s % HS, :]).then_inc(hid_lo_done, 1)
                    if first and s == 3:
                        ve.wait_ge(cw_rows_ready, 1)
                        nc.vector.tensor_copy(cw_rows[:], ps_cw).then_inc(cw_rows_done, 1)
                    if s % FT == 1 and not (first and s == 1):
                        i = (s - 1) // FT - 1
                        k, c = 2 * CH * e + i, i % CH
                        ve.wait_ge(down_ready, k + 1)
                        ve.wait_ge(cw_in[c], DMA * ((e if i >= 0 else e - 1) + 1))
                        fresh = first and 0 <= i < CH
                        if not fresh:
                            at_least(ve, acc_done, k - 2 - CH + 1)
                        dst = acc[:, :, c * TC:(c + 1) * TC] if fresh else part[:, c % 2, :, :]
                        nc.vector.tensor_tensor(dst, ps_d[c % 2], cw_all[:, None, c * TC:(c + 1) * TC].broadcast_to((P, DK, TC)),
                                                ALU.mult).then_inc(part_done, 1)

            expert(0, first=True)
            with ve.Fori(1, E - 1) as e:
                expert(e)
            expert(E - 1, last=True)

            for b in range(B):
                ve.wait_ge(y_ready, b + 1)
                nc.vector.tensor_tensor(xs[:, b, :], xs[:, b, :], ps[0:TQ, b % 4, 0:D], ALU.add).then_inc(y_done, 1)

        @block.tensor
        def _(pe):
            def transpose_norm(p):
                pe.wait_ge(xn_done, p + 1)
                for b in range(2):
                    for k in range(DK):
                        ins = nc.tensor.transpose(ps_x[:, k, b * TQ:(b + 1) * TQ], xn[:, b, k * P:(k + 1) * P], ident[0:TQ, 0:TQ])
                ins.then_inc(xt_ready, 1)

            def transpose_ctx(p, b):
                pe.wait_ge(ctx_in, DMA * (p + 1))
                at_least(pe, ct_lo_done, 2 * p + b)
                for k in range(DK):
                    for t in range(KT):
                        at = t * D + k * P
                        ins = nc.tensor.transpose(ps_c[:, k, t * KP:(t + 1) * KP], ctx_raw[:, b, at:at + P], ident[0:KP, 0:KP])
                ins.then_inc(ct_ready, 1)

            def queries(p):
                pe.wait_ge(xt_lo_done, p + 1)
                for j in range(DK):
                    cols = slice(j * P, (j + 1) * P)
                    accumulate(ps_x[:, j, :], [t for k in range(DK) for t in
                                               three(m_hi[:, k, cols], m_lo[:, k, cols], xt_hi[:, k, :], xt_lo[:, k, :])])
                for b in range(2):
                    rows = slice(b * TQ, (b + 1) * TQ)
                    ins = accumulate(ps_qb[:, b, :], [(xt[:, k, rows], v_split[:, k, :]) for k in range(DK) for xt in (xt_hi, xt_lo)])
                ins.then_inc(q_ready, 1)

            def scores(p, b):
                if b == 0:
                    pe.wait_ge(q_lo_done, p + 1)
                pe.wait_ge(ct_lo_done, 2 * p + b + 1)
                rows = slice(b * TQ, (b + 1) * TQ)
                accumulate(ps_s[b], [t for k in range(DK) for t in
                                     three(q_hi[:, k, rows], q_lo[:, k, rows], ct_hi[:, b, k, :], ct_lo[:, b, k, :])]).then_inc(scores_ready, 1)

            def transpose_probs(p, b):
                pe.wait_ge(probs_done, 2 * p + b + 1)
                for t in range(KT):
                    ins = nc.tensor.transpose(ps_p[b][:, t, :], probs[:, b, t * KP:(t + 1) * KP], ident[0:TQ, 0:TQ])
                ins.then_inc(pt_ready, 1)

            def mix_ctx(p):
                for b in range(2):
                    pe.wait_ge(pt_lo_done, 2 * p + b + 1)
                    pe.wait_ge(cn_lo_done, 2 * p + b + 1)
                    ins = accumulate(ps_a[:, b, :], [x for t in range(KT) for x in
                                                     three(pt_hi[:, b, t, :], pt_lo[:, b, t, :], cn_hi[:, b, t, :], cn_lo[:, b, t, :])])
                ins.then_inc(mix_ready, 1)

            def transpose_mix(p):
                pe.wait_ge(mix_done, p + 1)
                for b in range(2):
                    for k in range(DK):
                        ins = nc.tensor.transpose(ps_at[:, k, b * TQ:(b + 1) * TQ], mix[:, b, k * P:(k + 1) * P], ident[0:TQ, 0:TQ])
                ins.then_inc(at_ready, 1)

            def values(p):
                pe.wait_ge(at_lo_done, p + 1)
                at_least(pe, x1_done, p)
                for b in range(2):
                    rows = slice(b * TQ, (b + 1) * TQ)
                    ins = accumulate(ps_o[:, b, :], [t for k in range(DK) for t in
                                                     three(at_hi[:, k, rows], at_lo[:, k, rows], wv_hi[:, k, :], wv_lo[:, k, :])])
                ins.then_inc(o_ready, 1)

            def transpose_norm2(p):
                pe.wait_ge(xn2_done, p + 1)
                at_least(pe, logits_done, p)
                for b in range(2):
                    for k in range(DK):
                        ins = nc.tensor.transpose(ps_x2[:, k, b * TQ:(b + 1) * TQ], xn2[:, b, k * P:(k + 1) * P], ident[0:TQ, 0:TQ])
                ins.then_inc(x2t_ready, 1)

            def route(p):
                pe.wait_ge(st_lo_done, p + 1)
                for b in range(2):
                    rows = slice(b * TQ, (b + 1) * TQ)
                    ins = accumulate(ps_l[:, b, :], [t for k in range(DK) for t in
                                                     three(st_hi[:, k, rows], st_lo[:, k, rows], wr_hi[:, k, :], wr_lo[:, k, :])])
                ins.then_inc(logits_ready, 1)

            pe.wait_ge(consts_set, 1)
            for i in range(2):
                pe.wait_ge(weights_in, 3 * DMA)
                for et in range(DK):
                    for k in range(DK):
                        ins = nc.tensor.transpose(ps_wt[i][:, et, k * P:(k + 1) * P], wqk_raw[i][:, k, et * P:(et + 1) * P], ident[:])
                ins.then_inc(wt_ready, 1)
            transpose_norm(0)
            pe.wait_ge(wt_lo_done, 2)
            for it in range(DK):
                cols = slice(it * P, (it + 1) * P)
                ins = accumulate(ps_m[:, it, :], [t for et in range(DK) for t in
                                                  three(wqt_hi[:, et, cols], wqt_lo[:, et, cols], wkt_hi[:, et, :], wkt_lo[:, et, :])])
            ins.then_inc(m_ready, 1)
            transpose_ctx(0, 0)
            pe.wait_ge(prod_done, 1)
            for i, (hi, lo, bias) in enumerate(((wkt_hi, wkt_lo, bq_sb), (wqt_hi, wqt_lo, bk_sb))):
                for j in range(DK):
                    cols = slice(j * P, (j + 1) * P)
                    accumulate(ps_b[:, i * DK + j:i * DK + j + 1],
                               [(w[:, et, cols].bitcast(fp32), bias[:, et:et + 1]) for et in range(DK) for w in (hi, lo)])
            accumulate(ps_b[0:TQ, 2 * DK:2 * DK + 1], [(ones[:], bqk_prod[:, et:et + 1]) for et in range(DK)]).then_inc(vb_ready, 1)
            transpose_ctx(0, 1)
            pe.wait_ge(m_lo_done, 1)
            pe.wait_ge(vb_done, 1)
            queries(0)

            def pair(p, first=False, last=False):
                scores(p, 0)
                scores(p, 1)
                if not last:
                    transpose_norm(p + 1)
                    transpose_ctx(p + 1, 0)
                transpose_probs(p, 0)
                transpose_probs(p, 1)
                if not last:
                    transpose_ctx(p + 1, 1)
                mix_ctx(p)
                if not last:
                    queries(p + 1)
                transpose_mix(p)
                if not first:
                    transpose_norm2(p - 1)
                values(p)
                if not first:
                    route(p - 1)

            pe.wait_ge(wv_lo_done, 2)
            pair(0, first=True)
            with pe.Fori(1, PAIRS - 1) as p:
                pair(p)
            pair(PAIRS - 1, last=True)
            transpose_norm2(PAIRS - 1)
            route(PAIRS - 1)
            pe.wait_ge(logits_done, PAIRS)

            def expert(e, first=False, last=False):
                for s in range(STEPS + (LAG if last else 0)):
                    n = STEPS * e + s
                    if s < STEPS:
                        half, c, f = s // (CH * FT), s // FT % CH, s % FT
                        gate_hi, up_hi, _ = half_weights(w_hi, half)
                        gate_lo, up_lo, _ = half_weights(w_lo, half)
                        cols, toks = slice(f * P, (f + 1) * P), slice(c * TC, (c + 1) * TC)
                        if s % (CH * FT) == 0:
                            pe.wait_ge(w_done, 2 * e + half + 1)
                        if first and half == 0 and f == 0:
                            pe.wait_ge(h_in_done, 2 * DMA * PAIRS // CH * (c + 1))
                        at_least(pe, act_done, n - 1)
                        accumulate(ps_g[s % 2], [t for k in range(DK) for t in
                                                 three(gate_hi[:, k, cols], gate_lo[:, k, cols], h_in_hi[:, k, toks], h_in_lo[:, k, toks])]
                                   ).then_inc(gate_ready, 1)
                        at_least(pe, hid_done, n - 1)
                        accumulate(ps_u[s % 2], [t for k in range(DK) for t in
                                                 three(up_hi[:, k, cols], up_lo[:, k, cols], h_in_hi[:, k, toks], h_in_lo[:, k, toks])]
                                   ).then_inc(up_ready, 1)
                    if first and s == 3:
                        pe.wait_ge(cw_ready, 1)
                        nc.tensor.transpose(ps_cw, cw_t[:, :, :].rearrange("p e b -> p (e b)"), ident[0:TQ, 0:TQ]).then_inc(cw_rows_ready, 1)
                    if first and s < LAG:
                        continue
                    i = s - LAG
                    half, c, f, slot = i // (CH * FT) % HALVES, i // FT % CH, i % FT, i % HS
                    _, _, down_hi = half_weights(w_hi, half)
                    _, _, down_lo = half_weights(w_lo, half)
                    pe.wait_ge(hid_lo_done, n - LAG + 1)
                    if f == 0:
                        at_least(pe, part_done, 2 * CH * e + i // FT - 1)
                    if first and i == FT:
                        pe.wait_ge(cw_rows_done, 1)
                    for d in range(DK):
                        cols = slice(d * P, (d + 1) * P)
                        ins = accumulate(ps_d[c % 2][:, d, :],
                                         three(down_hi[:, f, cols], down_lo[:, f, cols], hs[:, 0, slot, :], hs[:, 1, slot, :]),
                                         first=f == 0, last=f == FT - 1)
                    if f == FT - 1:
                        ins.then_inc(down_ready, 1)

            expert(0, first=True)
            with pe.Fori(1, E - 1) as e:
                expert(e)
            expert(E - 1, last=True)

            for b in range(B):
                c = b // BC
                pe.wait_ge(acc_done, 2 * CH * E - 2 * CH + c + 1)
                at_least(pe, y_done, b - 3)
                for d in range(DK):
                    ins = nc.tensor.transpose(ps[0:TQ, b % 4, d * P:(d + 1) * P], acc[:, d, b * TQ:(b + 1) * TQ], ident[:])
                ins.then_inc(y_ready, 1)


_INS = ['x', 'ctx_1024', 'L0_xattn_Wq', 'L0_xattn_bq', 'L0_xattn_Wk', 'L0_xattn_bk', 'L0_xattn_Wv', 'L0_xattn_bv',
        'L0_ffn_w_router', 'L0_ffn_w_gating', 'L0_ffn_w_gate', 'L0_ffn_w_up', 'L0_ffn_w_down']


def kernel(**inputs):
    import numpy as _np
    import concourse.bacc as _bacc
    from concourse import mybir as _mybir
    from concourse.bass_utils import run_bass_kernel_spmd as _run

    nc = _bacc.Bacc("TRN2", target_bir_lowering=False, num_devices=1)
    arrays, args = {}, []
    for name in _INS:
        a = _np.ascontiguousarray(inputs[name])
        arrays[f"in_{name}"] = a
        args.append(nc.dram_tensor(f"in_{name}", a.shape, _mybir.dt.from_np(a.dtype), kind="ExternalInput").ap())
    shape = tuple(inputs['x'].shape)
    args.append(nc.dram_tensor("out_dram", shape, _mybir.dt.from_np(_np.dtype('float32')), kind="ExternalOutput").ap())
    xattn_ffn_kernel(nc, *args)
    return _run(nc, [arrays], core_ids=[0]).results[0]["out_dram"]
```

```python
import concourse.bass as bass
from concourse import mybir
from contextlib import ExitStack


def xattn_ffn_kernel(nc, x, ctx, wq, bq, wk, bk, wv, bv, w_router, w_gating, w_gate, w_up, w_down, out):
    fp32, fp32r = mybir.dt.float32, mybir.dt.float32r
    ALU, ACT, AX = mybir.AluOpType, mybir.ActivationFunctionType, mybir.AxisListType

    B, TQ, D = x.shape
    TK = ctx.shape[1]
    E, _, F = w_gate.shape
    P = 128
    DK = D // P
    KT = 3
    KP = TK // KT
    SK = TK + TK % 2
    PAIRS = B // 2
    TP = 2 * TQ
    T = B * TQ
    CH = 4
    TC = T // CH
    BC = B // CH
    HALVES = 2
    FH = F // HALVES
    FT = FH // P
    STEPS = HALVES * CH * FT
    LAG = 2
    HS = 4
    SCALE = float(D) ** -0.5
    EPS = 1e-5
    TEMP = 0.1
    DMA = 16

    x_v = x.rearrange("b q d -> q b d")
    out_v = out.rearrange("b q d -> q b d")
    ctx_v = ctx.rearrange("(n two) (p t) d -> n p two (t d)", two=2, t=KT)
    gate_v = w_gate.rearrange("e (k p) (h f) -> e h p k f", p=P, h=HALVES)
    up_v = w_up.rearrange("e (k p) (h f) -> e h p k f", p=P, h=HALVES)
    down_v = w_down.rearrange("e (h t p) d -> e h p t d", p=P, h=HALVES)
    cw_dram = nc.dram_tensor("cw_dram", (E, T), fp32).ap()

    es = ExitStack()
    with es:
        def sb(name, shape, dt=fp32):
            return es.enter_context(nc.sbuf_tensor(name, shape, dt))

        def sem(name):
            return es.enter_context(nc.semaphore(name))

        def at_least(engine, semaphore, count):
            if not isinstance(count, int) or count > 0:
                engine.wait_ge(semaphore, count)

        ident = sb("ident", [P, P])
        ones = sb("ones", [P, TQ])
        eps_c = sb("eps_c", [TQ, B])
        power_c = sb("power_c", [TQ, B])
        zero_c = sb("zero_c", [TQ, B])
        b_raw = sb("b_raw", [P, 2, DK])
        b_split = sb("b_split", [P, 2, DK, 2], fp32r)
        bqk_prod = sb("bqk_prod", [P, DK])
        qbias = sb("qbias", [P, DK])
        vb_sum = sb("vb_sum", [P, 2 * DK])
        v_split = sb("v_split", [P, DK, 2], fp32r)
        c0 = sb("c0", [TQ, 1])
        m_hi = sb("m_hi", [P, DK, D], fp32r)
        m_lo = sb("m_lo", [P, DK, D], fp32r)
        wv_hi = sb("wv_hi", [P, DK, D], fp32r)
        wv_lo = sb("wv_lo", [P, DK, D], fp32r)
        wr_raw = sb("wr_raw", [P, DK, 2 * E])
        wr_hi = sb("wr_hi", [P, DK, 2 * E], fp32r)
        wr_lo = sb("wr_lo", [P, DK, 2 * E], fp32r)
        xs = sb("xs", [TQ, B, D])
        h_in_hi = sb("h_in_hi", [P, DK, T], fp32r)
        h_in_lo = sb("h_in_lo", [P, DK, T], fp32r)
        w_raw = sb("w_raw", [P, 3, DK * FH])
        w_hi = sb("w_hi", [P, HALVES, 3, DK * FH], fp32r)
        w_lo = sb("w_lo", [P, HALVES, 3, DK * FH], fp32r)
        cn_hi, cn_lo = [w[0:KP, HALVES - 1, :, :].rearrange("p a n -> p (a n)")[:, 0:4 * KT * D]
                        .rearrange("p (s b t d) -> p s b t d", s=2, b=2, t=KT) for w in (w_hi, w_lo)]
        ct_hi = sb("ct_hi", [P, 2, DK, SK], fp32r)
        ct_lo = sb("ct_lo", [P, 2, DK, SK], fp32r)
        ctx_nat = sb("ctx_nat", [KP, 2, KT * D])
        xt_hi = sb("xt_hi", [P, DK, TP], fp32r)
        xt_lo = sb("xt_lo", [P, DK, TP], fp32r)
        q_hi = sb("q_hi", [P, DK, TP], fp32r)
        q_lo = sb("q_lo", [P, DK, TP], fp32r)
        pt_hi = sb("pt_hi", [KP, 2, KT, TQ], fp32r)
        pt_lo = sb("pt_lo", [KP, 2, KT, TQ], fp32r)
        st_hi = sb("st_hi", [P, DK, TP], fp32r)
        st_lo = sb("st_lo", [P, DK, TP], fp32r)
        bn1 = sb("bn1", [TQ, B, 6])
        mv1 = sb("mv1", [TQ, B, 2])
        bn2 = sb("bn2", [TQ, 2, 6])
        mv2 = sb("mv2", [TQ, 2, 2])
        var1, rstd1, shift1, bias1 = (sb(n, [TQ, B]) for n in ("var1", "rstd1", "shift1", "bias1"))
        var2, rstd2, shift2, bias2 = (sb(n, [TQ, 2]) for n in ("var2", "rstd2", "shift2", "bias2"))
        q_bk = sb("q_bk", [TQ, 2])
        top = sb("top", [TQ, 2])
        top_all = sb("top_all", [TQ, 2])
        neg_top = sb("neg_top", [TQ, 2])
        mass = sb("mass", [TQ, 2])
        inv_mass = sb("inv_mass", [TQ, 2])
        logits = sb("logits", [TQ, B, 2 * E])
        lg = sb("lg", [TQ, B * 2, E])
        lg_top = sb("lg_top", [TQ, B * 2])
        lg_sum = sb("lg_sum", [TQ, B * 2])
        cw = sb("cw", [TQ, B, E])
        cw_sum = sb("cw_sum", [TQ, B])
        cw_t = sb("cw_t", [TQ, E, B])
        cw_rows = sb("cw_rows", [P, TQ])
        cw_all = sb("cw_all", [P, T])
        acc = sb("acc", [P, DK, T])
        acc_f = acc[:, :, :].rearrange("p k t -> p (k t)")
        ctx_raw = acc_f[0:KP, 0:2 * KT * D].rearrange("p (b n) -> p b n", b=2)
        at0 = 2 * KT * D
        xn = acc_f[0:TQ, at0:at0 + 2 * D].rearrange("p (b n) -> p b n", b=2)
        at0 += 2 * D
        probs = acc_f[0:TQ, at0:at0 + 2 * TK].rearrange("p (b n) -> p b n", b=2)
        at0 += 2 * TK
        mix = acc_f[0:TQ, at0:at0 + 2 * D].rearrange("p (b n) -> p b n", b=2)
        part = sb("part", [P, 2, DK, TC])
        part_f = part[:, :, :, :].rearrange("p s k t -> p (s k t)")
        xn2 = part_f[0:TQ, 0:2 * D].rearrange("p (b n) -> p b n", b=2)
        bv_all = part_f[0:TQ, 2 * D:3 * D]
        hs = sb("hs", [P, 2, HS, TC], fp32r)
        hs_f = hs[:, :, :, :].rearrange("p a s t -> p (a s t)")
        wt = [hs_f[:, i * DK * D:(i + 1) * DK * D].rearrange("p (k n) -> p k n", k=DK) for i in range(4)]
        wqt_hi, wqt_lo, wkt_hi, wkt_lo = wt
        at0 = 4 * DK * D
        at_hi, at_lo = [hs_f[:, at0 + i * DK * TP:at0 + (i + 1) * DK * TP].rearrange("p (k n) -> p k n", k=DK)
                        for i in range(2)]
        wqk_raw = [sb(n, [P, DK, D]) for n in ("wq_raw", "wk_raw")]
        wv_raw = sb("wv_raw", [P, DK, D])
        act = sb("act", [P, 2, TC])
        hid = sb("hid", [P, 2, TC])

        ps = es.enter_context(nc.psum_tensor("ps", [P, 8, 512], fp32))
        ps_x = ps[:, 0, 0:DK * TP].rearrange("p (k t) -> p k t", k=DK)
        ps_qb = ps[0:TQ, 0, DK * TP:DK * TP + 4].rearrange("p (b n) -> p b n", b=2)
        ps_c = ps[:, 1:3, 0:TK]
        ps_s = [ps[0:TQ, 3 + b, 0:SK] for b in range(2)]
        ps_p = [ps[0:KP, 5 + b, 0:KT * TQ].rearrange("p (t q) -> p t q", t=KT) for b in range(2)]
        ps_a = ps[0:TQ, 5, :].rearrange("p (b n) -> p b n", b=2)
        ps_at = ps[:, 5, 0:DK * TP].rearrange("p (k t) -> p k t", k=DK)
        ps_o = ps[0:TQ, 6, :].rearrange("p (b n) -> p b n", b=2)
        ps_x2 = ps[:, 7, 0:DK * TP].rearrange("p (k t) -> p k t", k=DK)
        ps_l = ps[0:TQ, 7, DK * TP:DK * TP + 4 * E].rearrange("p (b n) -> p b n", b=2)
        ps_wt = [ps[:, 5 + i, :].rearrange("p (k n) -> p k n", k=DK) for i in range(2)]
        ps_m = ps[:, 3, :].rearrange("p (k n) -> p k n", k=DK)
        ps_b = ps[:, 4, 0:4 * DK].rearrange("p (a two) -> p a two", two=2)
        ps_c0 = ps[0:TQ, 4, 4 * DK:4 * DK + 1]
        ps_g = [ps[:, i, 0:TC] for i in range(2)]
        ps_u = [ps[:, 2 + i, 0:TC] for i in range(2)]
        ps_d = [ps[:, 4 + 2 * i:6 + 2 * i, 0:TC] for i in range(2)]
        ps_cw = ps[:, 6, 0:TQ]
        ps_y = [ps[0:TQ, 4 + 2 * i:6 + 2 * i, :] for i in range(2)]

        x_first, x_rest = sem("x_first"), sem("x_rest")
        weights_in, biases_in, router_in = sem("weights_in"), sem("biases_in"), sem("router_in")
        wv_in, bv_in = sem("wv_in"), sem("bv_in")
        zeros_set, consts_set = sem("zeros_set"), sem("consts_set")
        wt_ready, wt_hi_done, wt_lo_done = sem("wt_ready"), sem("wt_hi_done"), sem("wt_lo_done")
        m_ready, m_hi_done, m_lo_done = sem("m_ready"), sem("m_hi_done"), sem("m_lo_done")
        b_hi_done, b_split_done, vb_ready, vb_summed, v_hi_done, vb_done = (
            sem(n) for n in ("b_hi_done", "b_split_done", "vb_ready", "vb_summed", "v_hi_done", "vb_done"))
        wv_hi_done, wv_lo_done = sem("wv_hi_done"), sem("wv_lo_done")
        xt_ready, ct_ready, q_ready = sem("xt_ready"), sem("ct_ready"), sem("q_ready")
        scores_ready, pt_ready, mix_ready = sem("scores_ready"), sem("pt_ready"), sem("mix_ready")
        at_ready, o_ready, x2t_ready, logits_ready = sem("at_ready"), sem("o_ready"), sem("x2t_ready"), sem("logits_ready")
        xt_hi_done, ct_hi_done, q_hi_done, probs_done = sem("xt_hi_done"), sem("ct_hi_done"), sem("q_hi_done"), sem("probs_done")
        pt_hi_done, mix_done, at_hi_done, st_hi_done = sem("pt_hi_done"), sem("mix_done"), sem("at_hi_done"), sem("st_hi_done")
        xt_lo_done, ct_lo_done, q_lo_done, pt_lo_done = sem("xt_lo_done"), sem("ct_lo_done"), sem("q_lo_done"), sem("pt_lo_done")
        at_lo_done, st_lo_done = sem("at_lo_done"), sem("st_lo_done")
        stats1_done, xn_done = sem("stats1_done"), sem("xn_done")
        stats2_done, xn2_done = sem("stats2_done"), sem("xn2_done")
        top_done, top_all_done, neg_top_done, mass_inverted = sem("top_done"), sem("top_all_done"), sem("neg_top_done"), sem("mass_inverted")
        x1_done, logits_done = sem("x1_done"), sem("logits_done")
        norm_step, bias1_done, bias2_done = sem("norm_step"), sem("bias1_done"), sem("bias2_done")
        bv_added, cn_hi_done, cn_lo_done = sem("bv_added"), sem("cn_hi_done"), sem("cn_lo_done")
        ctx_in, nat_in, h_in_done = sem("ctx_in"), sem("nat_in"), sem("h_in_done")
        cw_step, lg_exp, cw_ready, cw_rows_ready, cw_rows_done, cw_stored = (
            sem(n) for n in ("cw_step", "lg_exp", "cw_ready", "cw_rows_ready", "cw_rows_done", "cw_stored"))
        cw_in = [sem(f"cw_in{c}") for c in range(CH)]
        w_in, w_hi_done, w_done = sem("w_in"), sem("w_hi_done"), sem("w_done")
        gate_ready, up_ready, down_ready = sem("gate_ready"), sem("up_ready"), sem("down_ready")
        act_done, hid_done, hid_hi_done, hid_lo_done = sem("act_done"), sem("hid_done"), sem("hid_hi_done"), sem("hid_lo_done")
        part_done, acc_done = sem("part_done"), sem("acc_done")
        y_ready, y_done, stored = sem("y_ready"), sem("y_done"), sem("stored")

        def inside(p):
            return not isinstance(p, int) or 0 <= p < PAIRS

        def three(w_high, w_low, m_high, m_low):
            return [(w_high, m_high), (w_high, m_low), (w_low, m_high)]

        def accumulate(dst, passes, first=True, last=True):
            for i, (w, m) in enumerate(passes):
                ins = nc.tensor.matmul(dst, w, m, start=first and i == 0, stop=last and i == len(passes) - 1)
            return ins

        def low(dst, src, high):
            return nc.vector.tensor_tensor(dst, src, high.bitcast(fp32), ALU.subtract)

        def half_weights(parts, half):
            gate = parts[:, half, 0, :].rearrange("p (k f) -> p k f", k=DK)
            up = parts[:, half, 1, :].rearrange("p (k f) -> p k f", k=DK)
            down = parts[:, half, 2, :].rearrange("p (t d) -> p t d", t=FT)
            return gate, up, down

        pieces = [(i, slice(j * 512, (j + 1) * 512)) for i in range(3) for j in range(DK * FH // 512)]

        block = es.enter_context(nc.Block())

        @block.sync
        def _(sp):
            for src, dst in ((wq, wqk_raw[0]), (wk, wqk_raw[1])):
                sp.dma_start(dst[:], src.rearrange("(k p) n -> p k n", p=P)).then_inc(weights_in, DMA)
            sp.dma_start(xs[:, 0:2, :], x_v[:, 0:2, :]).then_inc(x_first, DMA)
            with nc.allow_non_contiguous_dma("a few short rows"):
                for i, src in enumerate((bq, bk)):
                    sp.dma_start(b_raw[:, i, :], src.rearrange("(k p) -> p k", p=P)).then_inc(biases_in, DMA)
            sp.dma_start(ctx_raw, ctx_v[0]).then_inc(ctx_in, DMA)
            sp.dma_start(ctx_nat[:], ctx_v[0]).then_inc(nat_in, DMA)
            sp.dma_start(xs[:, 2:B, :], x_v[:, 2:B, :]).then_inc(x_rest, DMA)
            sp.dma_start(bv_all, bv[None, :].broadcast_to((TQ, D))).then_inc(bv_in, DMA)
            sp.dma_start(wv_raw[:], wv.rearrange("(k p) n -> p k n", p=P)).then_inc(wv_in, DMA)
            with nc.allow_non_contiguous_dma("a few short rows"):
                for i, src in enumerate((w_router, w_gating)):
                    sp.dma_start(wr_raw[:, :, i * E:(i + 1) * E], src.rearrange("(k p) n -> p k n", p=P)).then_inc(router_in, DMA)

            def load_ctx(p):
                sp.wait_ge(ct_ready, 2 * p)
                sp.dma_start(ctx_raw, ctx_v[p]).then_inc(ctx_in, DMA)

            def load_nat(p):
                sp.wait_ge(cn_lo_done, 2 * p)
                sp.dma_start(ctx_nat[:], ctx_v[p]).then_inc(nat_in, DMA)

            def keep_input(p):
                sp.wait_ge(st_hi_done, p + 1)
                sp.wait_ge(st_lo_done, p + 1)
                sp.dma_start(h_in_hi[:, :, bass.ds(p * TP, TP)].bitcast(fp32), st_hi[:, :, :].bitcast(fp32)).then_inc(h_in_done, DMA)
                sp.dma_start(h_in_lo[:, :, bass.ds(p * TP, TP)].bitcast(fp32), st_lo[:, :, :].bitcast(fp32)).then_inc(h_in_done, DMA)

            def load_weights(e, half):
                at_least(sp, w_done, 2 * e + half)
                for i, v in enumerate((gate_v, up_v)):
                    sp.dma_start(w_raw[:, i, :].rearrange("p (k f) -> p k f", k=DK), v[e, half]).then_inc(w_in, DMA)
                sp.dma_start(w_raw[:, 2, :].rearrange("p (t d) -> p t d", t=FT), down_v[e, half]).then_inc(w_in, DMA)

            def load_cw(e, c):
                sp.dma_start(cw_all[:, c * TC:(c + 1) * TC],
                             cw_dram[e, c * TC:(c + 1) * TC][None, :].broadcast_to((P, TC))).then_inc(cw_in[c], DMA)

            load_weights(0, 0)
            load_nat(1)
            load_ctx(1)
            load_ctx(2)
            load_nat(2)
            load_ctx(3)
            load_nat(3)
            with sp.Fori(2, PAIRS - 2) as p:
                load_ctx(p + 2)
                keep_input(p - 2)
                load_nat(p + 2)
            load_weights(0, 1)
            for p in range(PAIRS - 4, PAIRS):
                keep_input(p)
            sp.wait_ge(cw_rows_done, 1)
            sp.dma_start(cw_dram.rearrange("e (b t) -> (e b) t", t=TQ), cw_rows[:, :]).then_inc(cw_stored, DMA)
            sp.wait_ge(cw_stored, DMA)
            for c in range(CH):
                load_cw(0, c)
            with sp.Fori(0, E - 1) as e:
                load_weights(e + 1, 0)
                load_weights(e + 1, 1)
                for c in range(CH):
                    sp.wait_ge(part_done, 2 * CH * e + CH + c + 1)
                    load_cw(e + 1, c)
            for c in range(CH):
                sp.wait_ge(y_done, c + 1)
                sp.dma_start(out_v[:, c * BC:(c + 1) * BC, :], xs[:, c * BC:(c + 1) * BC, :]).then_inc(stored, DMA)
            sp.wait_ge(stored, DMA * CH)

        @block.gpsimd
        def _(pool):
            nc.gpsimd.memset(ident[:], 0.0).then_inc(zeros_set, 1)
            nc.gpsimd.memset(eps_c[:], EPS)
            nc.gpsimd.memset(power_c[:], -0.5)
            nc.gpsimd.memset(zero_c[:], 0.0)
            nc.gpsimd.memset(ones[:], 1.0)
            if SK > TK:
                for t in (ct_hi, ct_lo):
                    nc.gpsimd.memset(t[:, :, :, TK:SK].bitcast(fp32), 0.0)
            pool.wait_ge(zeros_set, 1)
            nc.gpsimd.affine_select(out=ident[:], in_=ident[:], compare_op=ALU.not_equal, fill=1.0, base=0,
                                    pattern=[[-1, P]], channel_multiplier=1).then_inc(consts_set, 1)
            pool.wait_ge(consts_set, 1)

            def norm_terms(mv, var, root, shift, bias, n, steps, done):
                nc.gpsimd.tensor_tensor(var, mv[:, :, 1], eps_c[:, 0:n], ALU.add).then_inc(norm_step, 1)
                pool.wait_ge(norm_step, steps + 1)
                nc.gpsimd.tensor_tensor(root, var, power_c[:, 0:n], ALU.pow).then_inc(norm_step, 1)
                pool.wait_ge(norm_step, steps + 2)
                nc.gpsimd.tensor_tensor(shift, mv[:, :, 0], root, ALU.mult).then_inc(norm_step, 1)
                pool.wait_ge(norm_step, steps + 3)
                nc.gpsimd.tensor_tensor(bias, zero_c[:, 0:n], shift, ALU.subtract).then_inc(done, 1)

            def norm2_terms(p):
                pool.wait_ge(stats2_done, p + 1)
                norm_terms(mv2[:], var2[:], rstd2[:], shift2[:], bias2[:], 2, 3 * (p + 2), bias2_done)

            def low_ctx(p):
                for b in range(2):
                    pool.wait_ge(cn_hi_done, 2 * p + b + 1)
                    nc.gpsimd.tensor_tensor(cn_lo[:, bass.ds(p % 2, 1), b, :, :], ctx_nat[:, b, :].rearrange("p (s t d) -> p s t d", s=1, t=KT),
                                            cn_hi[:, bass.ds(p % 2, 1), b, :, :].bitcast(fp32), ALU.subtract).then_inc(cn_lo_done, 1)

            def add_bv(p):
                pool.wait_ge(xn_done, p + 1)
                for b in range(2):
                    rows = xs[:, bass.ds(2 * p + b, 1), :]
                    ins = nc.gpsimd.tensor_tensor(rows, rows, bv_all[:, None, :], ALU.add)
                ins.then_inc(bv_added, 1)

            def low_weights(e, half):
                n = 2 * e + half
                pool.wait_ge(w_hi_done, n + 1)
                for i, s in pieces:
                    ins = nc.gpsimd.tensor_tensor(w_lo[:, half, i, s], w_raw[:, i, s], w_hi[:, half, i, s].bitcast(fp32), ALU.subtract)
                ins.then_inc(w_done, 1)

            def pair(p):
                if inside(p - 2):
                    norm2_terms(p - 2)
                if inside(p + 1):
                    add_bv(p + 1)
                    low_ctx(p + 1)

            for i, rows in enumerate((slice(0, 2), slice(2, B))):
                pool.wait_ge(stats1_done, i + 1)
                norm_terms(mv1[:, rows], var1[:, rows], rstd1[:, rows], shift1[:, rows], bias1[:, rows],
                           rows.stop - rows.start, 3 * i, bias1_done)
                if i == 0:
                    low_ctx(0)
            pool.wait_ge(bv_in, DMA)
            add_bv(0)
            pair(0)
            low_weights(0, 0)
            pair(1)
            with pool.Fori(2, PAIRS - 2) as p:
                pair(p)
            for p in range(PAIRS - 2, PAIRS + 2):
                pair(p)

            def add_part(k, c):
                pool.wait_ge(part_done, k + 1)
                at_least(pool, acc_done, k - 2 * CH + 1)
                a = acc[:, :, c * TC:(c + 1) * TC]
                nc.gpsimd.tensor_tensor(a, a, part[:, c % 2, :, :], ALU.add).then_inc(acc_done, 1)

            def expert(e, first=False, last=False):
                if not first:
                    add_part(2 * CH * e - 1, CH - 1)
                low_weights(e, 1)
                if not first:
                    for c in range(CH):
                        add_part(2 * CH * e + c, c)
                if not last:
                    low_weights(e + 1, 0)
                for c in range(CH - 1):
                    add_part(2 * CH * e + CH + c, c)

            expert(0, first=True)
            with pool.Fori(1, E - 1) as e:
                expert(e)
            expert(E - 1, last=True)

        @block.scalar
        def _(sc):
            def norm1(p):
                for b in range(2):
                    i = bass.ds(2 * p + b, 1)
                    ins = nc.scalar.activation(xn[:, b, :], xs[:, i, :], ACT.Identity, bias=bias1[:, i], scale=rstd1[:, i])
                ins.then_inc(xn_done, 1)

            def norm2(p):
                sc.wait_ge(bias2_done, p + 1)
                for b in range(2):
                    ins = nc.scalar.activation(xn2[:, b, :], xs[:, bass.ds(2 * p + b, 1), :], ACT.Identity,
                                               bias=bias2[:, b:b + 1], scale=rstd2[:, b:b + 1])
                ins.then_inc(xn2_done, 1)

            def xt_high(p):
                sc.wait_ge(xt_ready, p + 1)
                nc.scalar.copy(xt_hi[:], ps_x).then_inc(xt_hi_done, 1)

            def ct_high(p, b):
                sc.wait_ge(ct_ready, 2 * p + b + 1)
                nc.scalar.copy(ct_hi[:, b, :, 0:TK], ps_c).then_inc(ct_hi_done, 1)

            def q_high(p):
                sc.wait_ge(q_ready, p + 1)
                for j in range(DK):
                    ins = nc.scalar.activation(q_hi[:, j, :], ps_x[:, j, :], ACT.Identity, bias=qbias[:, j:j + 1])
                ins.then_inc(q_hi_done, 1)

            def exponentials(p):
                sc.wait_ge(neg_top_done, p + 1)
                for b in range(2):
                    nc.scalar.activation(probs[:, b, :], ps_s[b][:, 0:TK], ACT.Exp, bias=neg_top[:, b:b + 1],
                                         accum_out=mass[:, b:b + 1]).then_inc(probs_done, 1)

            def pt_high(p, b):
                sc.wait_ge(pt_ready, 2 * p + b + 1)
                nc.scalar.copy(pt_hi[:, b, :, :], ps_p[b]).then_inc(pt_hi_done, 1)

            def normalise(p):
                sc.wait_ge(mix_ready, p + 1)
                sc.wait_ge(mass_inverted, p + 1)
                for b in range(2):
                    ins = nc.scalar.activation(mix[:, b, :], ps_a[:, b, :], ACT.Identity, scale=inv_mass[:, b:b + 1])
                ins.then_inc(mix_done, 1)

            def at_high(p):
                sc.wait_ge(at_ready, p + 1)
                nc.scalar.copy(at_hi, ps_at).then_inc(at_hi_done, 1)

            def st_high(p):
                sc.wait_ge(x2t_ready, p + 1)
                at_least(sc, h_in_done, 2 * DMA * p)
                nc.scalar.copy(st_hi[:], ps_x2).then_inc(st_hi_done, 1)

            def cn_high(p):
                sc.wait_ge(nat_in, DMA * (p + 1))
                at_least(sc, mix_ready, p - 1)
                for b in range(2):
                    nc.scalar.copy(cn_hi[:, bass.ds(p % 2, 1), b, :, :],
                                   ctx_nat[:, b, :].rearrange("p (s t d) -> p s t d", s=1, t=KT)).then_inc(cn_hi_done, 1)

            def high_weights(e, half):
                n = 2 * e + half
                sc.wait_ge(w_in, 3 * DMA * (n + 1))
                at_least(sc, down_ready, CH * (n - 1))
                for i, s in pieces:
                    ins = nc.scalar.copy(w_hi[:, half, i, s], w_raw[:, i, s])
                ins.then_inc(w_hi_done, 1)

            for i, hi in enumerate((wqt_hi, wkt_hi)):
                sc.wait_ge(wt_ready, i + 1)
                nc.scalar.copy(hi, ps_wt[i]).then_inc(wt_hi_done, 1)
            sc.wait_ge(bias1_done, 1)
            norm1(0)
            ct_high(0, 0)
            xt_high(0)
            cn_high(0)
            sc.wait_ge(m_ready, 1)
            nc.scalar.mul(m_hi[:], ps_m, SCALE).then_inc(m_hi_done, 1)
            ct_high(0, 1)
            high_weights(0, 0)
            sc.wait_ge(vb_done, 1)
            q_high(0)
            sc.wait_ge(wv_in, DMA)
            nc.scalar.copy(wv_hi[:], wv_raw[:]).then_inc(wv_hi_done, 1)
            sc.wait_ge(router_in, 2 * DMA)
            nc.scalar.copy(wr_hi[:], wr_raw[:]).then_inc(wv_hi_done, 1)
            sc.wait_ge(bias1_done, 2)
            norm1(1)

            def pair(p):
                if inside(p - 1):
                    pt_high(p - 1, 0)
                    pt_high(p - 1, 1)
                if inside(p):
                    exponentials(p)
                if inside(p + 1):
                    xt_high(p + 1)
                    ct_high(p + 1, 0)
                if inside(p - 1):
                    normalise(p - 1)
                if inside(p - 2):
                    norm2(p - 2)
                if inside(p + 1):
                    ct_high(p + 1, 1)
                if inside(p - 1):
                    at_high(p - 1)
                if inside(p + 1):
                    cn_high(p + 1)
                    q_high(p + 1)
                if inside(p - 2):
                    st_high(p - 2)
                if inside(p + 2):
                    norm1(p + 2)

            pair(0)
            pair(1)
            with sc.Fori(2, PAIRS - 2) as p:
                pair(p)
            for p in range(PAIRS - 2, PAIRS + 2):
                pair(p)

            def expert(e, first=False, last=False):
                for s in range(STEPS):
                    n = STEPS * e + s
                    if first and s == LAG:
                        sc.wait_ge(cw_step, 2)
                        lgv = lg[:, :, :].rearrange("p (b two) e -> p b two e", two=2)
                        nc.scalar.activation(lgv[:, :, 0, :], lgv[:, :, 0, :], ACT.Exp)
                        nc.scalar.activation(lgv[:, :, 1, :], lgv[:, :, 1, :], ACT.Exp, scale=1.0 / TEMP).then_inc(lg_exp, 1)
                    if s == (2 * LAG if first else LAG):
                        high_weights(e, 1)
                    if s == STEPS // 2 + LAG and not last:
                        high_weights(e + 1, 0)
                    sc.wait_ge(gate_ready, n + 1)
                    at_least(sc, hid_done, n - 1)
                    nc.scalar.activation(act[:, s % 2, :], ps_g[s % 2], ACT.Silu).then_inc(act_done, 1)
                    sc.wait_ge(hid_done, n + 1)
                    nc.scalar.copy(hs[:, 0, s % HS, :], hid[:, s % 2, :]).then_inc(hid_hi_done, 1)

            expert(0, first=True)
            with sc.Fori(1, E - 1) as e:
                expert(e)
            expert(E - 1, last=True)

        @block.vector
        def _(ve):
            def stats1(first, end):
                for b in range(first, end):
                    nc.vector.bn_stats(bn1[:, b, :], xs[:, b, :])
                nc.vector.drain()
                for b in range(first, end):
                    ins = nc.vector.bn_aggr(mv1[:, b, :], bn1[:, b, :])
                if end in (2, B):
                    ins.then_inc(stats1_done, 1)

            def xt_low(p):
                ve.wait_ge(xt_hi_done, p + 1)
                low(xt_lo[:], ps_x, xt_hi[:]).then_inc(xt_lo_done, 1)

            def ct_low(p, b):
                ve.wait_ge(ct_hi_done, 2 * p + b + 1)
                low(ct_lo[:, b, :, 0:TK], ps_c, ct_hi[:, b, :, 0:TK]).then_inc(ct_lo_done, 1)

            def q_low(p):
                ve.wait_ge(q_hi_done, p + 1)
                nc.vector.tensor_reduce(q_bk[:], ps_qb, AX.X, ALU.add)
                for j in range(DK):
                    ins = nc.vector.scalar_tensor_tensor(q_lo[:, j, :], ps_x[:, j, :], qbias[:, j:j + 1],
                                                         q_hi[:, j, :].bitcast(fp32), ALU.add, ALU.subtract)
                ins.then_inc(q_lo_done, 1)

            def maxima(p):
                for b in range(2):
                    ve.wait_ge(scores_ready, 2 * p + b + 1)
                    ins = nc.vector.tensor_reduce(top[:, b:b + 1], ps_s[b][:, 0:TK], AX.X, ALU.max)
                ins.then_inc(top_done, 1)
                ve.wait_ge(q_lo_done, p + 1)
                ve.wait_ge(top_done, p + 1)
                nc.vector.scalar_tensor_tensor(top_all[:], q_bk[:], c0[:, 0:1], top[:], ALU.add, ALU.add).then_inc(top_all_done, 1)
                ve.wait_ge(top_all_done, p + 1)
                nc.vector.scalar_tensor_tensor(neg_top[:], q_bk[:], c0[:, 0:1], top_all[:], ALU.add, ALU.subtract).then_inc(neg_top_done, 1)

            def pt_low(p, b):
                ve.wait_ge(pt_hi_done, 2 * p + b + 1)
                low(pt_lo[:, b, :, :], ps_p[b], pt_hi[:, b, :, :]).then_inc(pt_lo_done, 1)

            def invert_mass(p):
                ve.wait_ge(probs_done, 2 * p + 2)
                nc.vector.reciprocal(inv_mass[:], mass[:]).then_inc(mass_inverted, 1)

            def at_low(p):
                ve.wait_ge(at_hi_done, p + 1)
                low(at_lo, ps_at, at_hi).then_inc(at_lo_done, 1)

            def st_low(p):
                ve.wait_ge(st_hi_done, p + 1)
                low(st_lo[:], ps_x2, st_hi[:]).then_inc(st_lo_done, 1)

            def residual1(p):
                ve.wait_ge(o_ready, p + 1)
                ve.wait_ge(bv_added, p + 1)
                rows = xs[:, bass.ds(2 * p, 2), :]
                nc.vector.tensor_tensor(rows, rows, ps_o, ALU.add).then_inc(x1_done, 1)

            def stats2(p):
                ve.wait_ge(x1_done, p + 1)
                ve.wait_ge(o_ready, p + 1)
                for b in range(2):
                    ins = nc.vector.bn_stats(bn2[:, b, :], xs[:, bass.ds(2 * p + b, 1), :])
                nc.vector.drain()
                for b in range(2):
                    ins = nc.vector.bn_aggr(mv2[:, b, :], bn2[:, b, :])
                ins.then_inc(stats2_done, 1)

            def keep_logits(p):
                ve.wait_ge(logits_ready, p + 1)
                nc.vector.tensor_copy(logits[:, bass.ds(2 * p, 2), :], ps_l).then_inc(logits_done, 1)

            ve.wait_ge(x_first, DMA)
            stats1(0, 2)
            ve.wait_ge(biases_in, 2 * DMA)
            nc.vector.tensor_copy(b_split[:, :, :, 0], b_raw[:])
            nc.vector.tensor_tensor(bqk_prod[:], b_raw[:, 0, :], b_raw[:, 1, :], ALU.mult).then_inc(b_hi_done, 1)
            ve.wait_ge(b_hi_done, 1)
            low(b_split[:, :, :, 1], b_raw[:], b_split[:, :, :, 0]).then_inc(b_split_done, 1)
            for i, (hi, lo) in enumerate(((wqt_hi, wqt_lo), (wkt_hi, wkt_lo))):
                ve.wait_ge(wt_hi_done, i + 1)
                low(lo, ps_wt[i], hi).then_inc(wt_lo_done, 1)
            ct_low(0, 0)
            xt_low(0)
            ve.wait_ge(m_hi_done, 1)
            nc.vector.scalar_tensor_tensor(m_lo[:], ps_m, SCALE, m_hi[:].bitcast(fp32), ALU.mult, ALU.subtract).then_inc(m_lo_done, 1)
            ve.wait_ge(x_rest, DMA)
            stats1(2, 6)
            ve.wait_ge(vb_ready, 1)
            nc.vector.tensor_scalar(c0[:], ps_c0, SCALE, None, ALU.mult)
            nc.vector.tensor_reduce(vb_sum[:], ps_b, AX.X, ALU.add).then_inc(vb_summed, 1)
            ve.wait_ge(vb_summed, 1)
            nc.vector.tensor_scalar(qbias[:], vb_sum[:, 0:DK], SCALE, None, ALU.mult)
            nc.vector.tensor_scalar(v_split[:, :, 0], vb_sum[:, DK:2 * DK], SCALE, None, ALU.mult).then_inc(v_hi_done, 1)
            ve.wait_ge(v_hi_done, 1)
            nc.vector.scalar_tensor_tensor(v_split[:, :, 1], vb_sum[:, DK:2 * DK], SCALE, v_split[:, :, 0].bitcast(fp32),
                                           ALU.mult, ALU.subtract).then_inc(vb_done, 1)
            stats1(6, 10)
            ct_low(0, 1)
            stats1(10, B)
            q_low(0)
            ve.wait_ge(wv_hi_done, 2)
            low(wv_lo[:], wv_raw[:], wv_hi[:]).then_inc(wv_lo_done, 1)
            low(wr_lo[:], wr_raw[:], wr_hi[:]).then_inc(wv_lo_done, 1)

            def pair(p):
                if inside(p - 1):
                    invert_mass(p - 1)
                    pt_low(p - 1, 0)
                    pt_low(p - 1, 1)
                if inside(p):
                    maxima(p)
                if inside(p - 2):
                    stats2(p - 2)
                if inside(p + 1):
                    xt_low(p + 1)
                    ct_low(p + 1, 0)
                    ct_low(p + 1, 1)
                if inside(p - 1):
                    at_low(p - 1)
                if inside(p + 1):
                    q_low(p + 1)
                if inside(p - 2):
                    st_low(p - 2)
                if inside(p - 1):
                    residual1(p - 1)
                if inside(p - 2):
                    keep_logits(p - 2)

            pair(0)
            pair(1)
            with ve.Fori(2, PAIRS - 2) as p:
                pair(p)
            for p in range(PAIRS - 2, PAIRS + 2):
                pair(p)

            lv = logits[:, :, :].rearrange("p b (two e) -> p (b two) e", two=2)
            ve.wait_ge(logits_done, PAIRS)
            nc.vector.tensor_reduce(lg_top[:], lv, AX.X, ALU.max).then_inc(cw_step, 1)
            ve.wait_ge(cw_step, 1)
            nc.vector.tensor_tensor(lg[:], lv, lg_top[:, :, None].broadcast_to((TQ, 2 * B, E)), ALU.subtract).then_inc(cw_step, 1)

            def token_weights():
                ve.wait_ge(lg_exp, 1)
                nc.vector.tensor_reduce(lg_sum[:], lg[:], AX.X, ALU.add).then_inc(cw_step, 1)
                ve.wait_ge(cw_step, 3)
                nc.vector.reciprocal(lg_top[:], lg_sum[:]).then_inc(cw_step, 1)
                ve.wait_ge(cw_step, 4)
                nc.vector.tensor_tensor(lg[:], lg[:], lg_top[:, :, None].broadcast_to((TQ, 2 * B, E)), ALU.mult).then_inc(cw_step, 1)
                ve.wait_ge(cw_step, 5)
                lgv = lg[:, :, :].rearrange("p (b two) e -> p b two e", two=2)
                nc.vector.tensor_tensor(cw[:], lgv[:, :, 0, :], lgv[:, :, 1, :], ALU.mult).then_inc(cw_step, 1)
                ve.wait_ge(cw_step, 6)
                nc.vector.tensor_reduce(cw_sum[:], cw[:], AX.X, ALU.add).then_inc(cw_step, 1)
                ve.wait_ge(cw_step, 7)
                nc.vector.tensor_scalar(cw_sum[:], cw_sum[:], 1e-9, None, ALU.add).then_inc(cw_step, 1)
                ve.wait_ge(cw_step, 8)
                nc.vector.reciprocal(lg_sum[:, 0:B], cw_sum[:]).then_inc(cw_step, 1)
                ve.wait_ge(cw_step, 9)
                nc.vector.tensor_tensor(cw_t[:, :, :].rearrange("p e b -> p b e"), cw[:],
                                        lg_sum[:, 0:B, None].broadcast_to((TQ, B, E)), ALU.mult).then_inc(cw_ready, 1)

            def expert(e, first=False, last=False):
                for s in range(STEPS + (LAG if last else 0)):
                    n = STEPS * e + s
                    if s < STEPS:
                        ve.wait_ge(act_done, n + 1)
                        ve.wait_ge(up_ready, n + 1)
                        at_least(ve, hid_hi_done, n - 1)
                        nc.vector.tensor_tensor(hid[:, s % 2, :], act[:, s % 2, :], ps_u[s % 2], ALU.mult).then_inc(hid_done, 1)
                        ve.wait_ge(hid_hi_done, n + 1)
                        low(hs[:, 1, s % HS, :], hid[:, s % 2, :], hs[:, 0, s % HS, :]).then_inc(hid_lo_done, 1)
                    if first and s == LAG:
                        token_weights()
                    if first and s == FT:
                        ve.wait_ge(cw_rows_ready, 1)
                        nc.vector.tensor_copy(cw_rows[:], ps_cw).then_inc(cw_rows_done, 1)
                    turn = 2 * FT if first and s == 2 * FT else s - 1 if s % FT == 1 and not (first and s in (1, FT + 1)) else None
                    if turn is not None:
                        i = 0 if s == 2 * FT else turn // FT - 1
                        k, c = 2 * CH * e + i, i % CH
                        ve.wait_ge(down_ready, k + 1)
                        ve.wait_ge(cw_in[c], DMA * ((e if i >= 0 else e - 1) + 1))
                        fresh = first and 0 <= i < CH
                        if not fresh:
                            at_least(ve, acc_done, k - 2 - CH + 1)
                        dst = acc[:, :, c * TC:(c + 1) * TC] if fresh else part[:, c % 2, :, :]
                        nc.vector.tensor_tensor(dst, ps_d[c % 2], cw_all[:, None, c * TC:(c + 1) * TC].broadcast_to((P, DK, TC)),
                                                ALU.mult).then_inc(part_done, 1)
                        if last and i == 2 * CH - 1:
                            ve.wait_ge(part_done, k + 1)
                            ve.wait_ge(acc_done, k - 2 * CH + 1)
                            a = acc[:, :, c * TC:(c + 1) * TC]
                            nc.vector.tensor_tensor(a, a, part[:, c % 2, :, :], ALU.add).then_inc(acc_done, 1)
                    if last and s >= STEPS // 2 + 2 * FT and s % FT == 0:
                        residual2((s - STEPS // 2) // FT - 2)

            def residual2(c):
                ve.wait_ge(y_ready, c + 1)
                rows = xs[:, c * BC:(c + 1) * BC, :].rearrange("p (k b) d -> p k (b d)", k=DK)
                nc.vector.tensor_tensor(rows, rows, ps_y[c % 2], ALU.add).then_inc(y_done, 1)

            expert(0, first=True)
            with ve.Fori(1, E - 1) as e:
                expert(e)
            expert(E - 1, last=True)

            residual2(CH - 1)

        @block.tensor
        def _(pe):
            def transpose_norm(p):
                pe.wait_ge(xn_done, p + 1)
                for b in range(2):
                    for k in range(DK):
                        ins = nc.tensor.transpose(ps_x[:, k, b * TQ:(b + 1) * TQ], xn[:, b, k * P:(k + 1) * P], ident[0:TQ, 0:TQ])
                ins.then_inc(xt_ready, 1)

            def transpose_ctx(p, b):
                pe.wait_ge(ctx_in, DMA * (p + 1))
                at_least(pe, ct_lo_done, 2 * p + b)
                for k in range(DK):
                    for t in range(KT):
                        at = t * D + k * P
                        ins = nc.tensor.transpose(ps_c[:, k, t * KP:(t + 1) * KP], ctx_raw[:, b, at:at + P], ident[0:KP, 0:KP])
                ins.then_inc(ct_ready, 1)

            def queries(p):
                pe.wait_ge(xt_lo_done, p + 1)
                for j in range(DK):
                    cols = slice(j * P, (j + 1) * P)
                    accumulate(ps_x[:, j, :], [t for k in range(DK) for t in
                                               three(m_hi[:, k, cols], m_lo[:, k, cols], xt_hi[:, k, :], xt_lo[:, k, :])])
                for b in range(2):
                    rows = slice(b * TQ, (b + 1) * TQ)
                    ins = accumulate(ps_qb[:, b, :], [(xt[:, k, rows], v_split[:, k, :]) for k in range(DK) for xt in (xt_hi, xt_lo)])
                ins.then_inc(q_ready, 1)

            def scores(p, b):
                if b == 0:
                    pe.wait_ge(q_lo_done, p + 1)
                pe.wait_ge(ct_lo_done, 2 * p + b + 1)
                rows = slice(b * TQ, (b + 1) * TQ)
                accumulate(ps_s[b], [t for k in range(DK) for t in
                                     three(q_hi[:, k, rows], q_lo[:, k, rows], ct_hi[:, b, k, :], ct_lo[:, b, k, :])]).then_inc(scores_ready, 1)

            def transpose_probs(p, b):
                pe.wait_ge(probs_done, 2 * p + b + 1)
                if b == 1:
                    at_least(pe, x1_done, p)
                for t in range(KT):
                    ins = nc.tensor.transpose(ps_p[b][:, t, :], probs[:, b, t * KP:(t + 1) * KP], ident[0:TQ, 0:TQ])
                ins.then_inc(pt_ready, 1)

            def mix_ctx(p):
                for b in range(2):
                    pe.wait_ge(pt_lo_done, 2 * p + b + 1)
                    pe.wait_ge(cn_lo_done, 2 * p + b + 1)
                    ins = accumulate(ps_a[:, b, :], [x for t in range(KT) for x in
                                                     three(pt_hi[:, b, t, :], pt_lo[:, b, t, :], cn_hi[:, p % 2, b, t, :], cn_lo[:, p % 2, b, t, :])])
                ins.then_inc(mix_ready, 1)

            def transpose_mix(p):
                pe.wait_ge(mix_done, p + 1)
                for b in range(2):
                    for k in range(DK):
                        ins = nc.tensor.transpose(ps_at[:, k, b * TQ:(b + 1) * TQ], mix[:, b, k * P:(k + 1) * P], ident[0:TQ, 0:TQ])
                ins.then_inc(at_ready, 1)

            def values(p):
                pe.wait_ge(at_lo_done, p + 1)
                for b in range(2):
                    rows = slice(b * TQ, (b + 1) * TQ)
                    ins = accumulate(ps_o[:, b, :], [t for k in range(DK) for t in
                                                     three(at_hi[:, k, rows], at_lo[:, k, rows], wv_hi[:, k, :], wv_lo[:, k, :])])
                ins.then_inc(o_ready, 1)

            def transpose_norm2(p):
                pe.wait_ge(xn2_done, p + 1)
                at_least(pe, logits_done, p)
                for b in range(2):
                    for k in range(DK):
                        ins = nc.tensor.transpose(ps_x2[:, k, b * TQ:(b + 1) * TQ], xn2[:, b, k * P:(k + 1) * P], ident[0:TQ, 0:TQ])
                ins.then_inc(x2t_ready, 1)

            def route(p):
                pe.wait_ge(st_lo_done, p + 1)
                for b in range(2):
                    rows = slice(b * TQ, (b + 1) * TQ)
                    ins = accumulate(ps_l[:, b, :], [t for k in range(DK) for t in
                                                     three(st_hi[:, k, rows], st_lo[:, k, rows], wr_hi[:, k, :], wr_lo[:, k, :])])
                ins.then_inc(logits_ready, 1)

            pe.wait_ge(consts_set, 1)
            pe.wait_ge(weights_in, 2 * DMA)
            for i in range(2):
                for et in range(DK):
                    for k in range(DK):
                        ins = nc.tensor.transpose(ps_wt[i][:, et, k * P:(k + 1) * P], wqk_raw[i][:, k, et * P:(et + 1) * P], ident[:])
                ins.then_inc(wt_ready, 1)
            transpose_ctx(0, 0)
            transpose_norm(0)
            pe.wait_ge(wt_lo_done, 2)
            for it in range(DK):
                cols = slice(it * P, (it + 1) * P)
                ins = accumulate(ps_m[:, it, :], [t for et in range(DK) for t in
                                                  three(wqt_hi[:, et, cols], wqt_lo[:, et, cols], wkt_hi[:, et, :], wkt_lo[:, et, :])])
            ins.then_inc(m_ready, 1)
            pe.wait_ge(b_split_done, 1)
            for i, ws in enumerate(((wkt_hi, wkt_lo), (wqt_hi, wqt_lo))):
                for j in range(DK):
                    cols = slice(j * P, (j + 1) * P)
                    accumulate(ps_b[:, i * DK + j, :], [(w[:, et, cols], b_split[:, i, et, :]) for et in range(DK) for w in ws])
            accumulate(ps_c0, [(ones[:], bqk_prod[:, et:et + 1]) for et in range(DK)]).then_inc(vb_ready, 1)
            transpose_ctx(0, 1)
            pe.wait_ge(m_lo_done, 1)
            pe.wait_ge(vb_done, 1)
            queries(0)

            def pair(p):
                if inside(p - 1):
                    transpose_probs(p - 1, 0)
                    transpose_probs(p - 1, 1)
                if inside(p):
                    scores(p, 0)
                    scores(p, 1)
                if inside(p + 1):
                    transpose_norm(p + 1)
                    transpose_ctx(p + 1, 0)
                if inside(p - 1):
                    mix_ctx(p - 1)
                if inside(p + 1):
                    transpose_ctx(p + 1, 1)
                if inside(p - 1):
                    transpose_mix(p - 1)
                if inside(p + 1):
                    queries(p + 1)
                if inside(p - 2):
                    transpose_norm2(p - 2)
                if inside(p - 1):
                    values(p - 1)
                if inside(p - 2):
                    route(p - 2)

            def gate_up(e, s, first=False):
                n = STEPS * e + s
                half, c, f = s // (CH * FT), s // FT % CH, s % FT
                gate_hi, up_hi, _ = half_weights(w_hi, half)
                gate_lo, up_lo, _ = half_weights(w_lo, half)
                cols, toks = slice(f * P, (f + 1) * P), slice(c * TC, (c + 1) * TC)
                if s % (CH * FT) == 0:
                    pe.wait_ge(w_done, 2 * e + half + 1)
                if first and half == 0 and f == 0:
                    pe.wait_ge(h_in_done, 2 * DMA * PAIRS // CH * (c + 1))
                at_least(pe, act_done, n - 1)
                accumulate(ps_g[s % 2], [t for k in range(DK) for t in
                                         three(gate_hi[:, k, cols], gate_lo[:, k, cols], h_in_hi[:, k, toks], h_in_lo[:, k, toks])]
                           ).then_inc(gate_ready, 1)
                at_least(pe, hid_done, n - 1)
                accumulate(ps_u[s % 2], [t for k in range(DK) for t in
                                         three(up_hi[:, k, cols], up_lo[:, k, cols], h_in_hi[:, k, toks], h_in_lo[:, k, toks])]
                           ).then_inc(up_ready, 1)

            def down(e, i, last=False):
                half, c, f, slot = i // (CH * FT) % HALVES, i // FT % CH, i % FT, i % HS
                _, _, down_hi = half_weights(w_hi, half)
                _, _, down_lo = half_weights(w_lo, half)
                pe.wait_ge(hid_lo_done, STEPS * e + i + 1)
                if f == 0:
                    at_least(pe, part_done, 2 * CH * e + i // FT - 1)
                    if last and half == HALVES - 1 and c >= 2:
                        pe.wait_ge(y_done, c - 1)
                for d in range(DK):
                    cols = slice(d * P, (d + 1) * P)
                    ins = accumulate(ps_d[c % 2][:, d, :],
                                     three(down_hi[:, f, cols], down_lo[:, f, cols], hs[:, 0, slot, :], hs[:, 1, slot, :]),
                                     first=f == 0, last=f == FT - 1)
                if f == FT - 1:
                    ins.then_inc(down_ready, 1)

            def sum_rows(c):
                pe.wait_ge(acc_done, 2 * CH * E - 2 * CH + c + 1)
                for j in range(BC):
                    b, bank, at = c * BC + j, j * D // 512, j * D % 512
                    for d in range(DK):
                        ins = nc.tensor.transpose(ps_y[c % 2][:, bank, at + d * P:at + (d + 1) * P], acc[:, d, b * TQ:(b + 1) * TQ], ident[:])
                ins.then_inc(y_ready, 1)

            def expert(e, first=False, last=False):
                for s in range(STEPS + (LAG if last else 0)):
                    if s < STEPS and not (first and s < LAG):
                        gate_up(e, s, first)
                    if first and s == FT:
                        pe.wait_ge(cw_ready, 1)
                        pe.wait_ge(logits_done, PAIRS)
                        nc.tensor.transpose(ps_cw, cw_t[:, :, :].rearrange("p e b -> p (e b)"), ident[0:TQ, 0:TQ]).then_inc(cw_rows_ready, 1)
                    if first and s == LAG + FT:
                        pe.wait_ge(cw_rows_done, 1)
                    if not (first and s < LAG):
                        down(e, s - LAG, last)
                    if last and s >= STEPS // 2 + 2 * FT and s % FT == 0:
                        sum_rows((s - STEPS // 2) // FT - 2)

            pair(0)
            pe.wait_ge(wv_lo_done, 2)
            pair(1)
            with pe.Fori(2, PAIRS - 2) as p:
                pair(p)
            for p in range(PAIRS - 2, PAIRS):
                pair(p)
            transpose_probs(PAIRS - 1, 0)
            transpose_probs(PAIRS - 1, 1)
            gate_up(0, 0, first=True)
            mix_ctx(PAIRS - 1)
            transpose_norm2(PAIRS - 2)
            transpose_mix(PAIRS - 1)
            values(PAIRS - 1)
            route(PAIRS - 2)
            gate_up(0, 1)
            transpose_norm2(PAIRS - 1)
            route(PAIRS - 1)

            expert(0, first=True)
            with pe.Fori(1, E - 1) as e:
                expert(e)
            expert(E - 1, last=True)
            sum_rows(CH - 1)


_INS = ['x', 'ctx_1024', 'L0_xattn_Wq', 'L0_xattn_bq', 'L0_xattn_Wk', 'L0_xattn_bk', 'L0_xattn_Wv', 'L0_xattn_bv',
        'L0_ffn_w_router', 'L0_ffn_w_gating', 'L0_ffn_w_gate', 'L0_ffn_w_up', 'L0_ffn_w_down']


def kernel(**inputs):
    import numpy as _np
    import concourse.bacc as _bacc
    from concourse import mybir as _mybir
    from concourse.bass_utils import run_bass_kernel_spmd as _run

    nc = _bacc.Bacc("TRN2", target_bir_lowering=False, num_devices=1)
    arrays, args = {}, []
    for name in _INS:
        a = _np.ascontiguousarray(inputs[name])
        arrays[f"in_{name}"] = a
        args.append(nc.dram_tensor(f"in_{name}", a.shape, _mybir.dt.from_np(a.dtype), kind="ExternalInput").ap())
    shape = tuple(inputs['x'].shape)
    args.append(nc.dram_tensor("out_dram", shape, _mybir.dt.from_np(_np.dtype('float32')), kind="ExternalOutput").ap())
    xattn_ffn_kernel(nc, *args)
    return _run(nc, [arrays], core_ids=[0]).results[0]["out_dram"]
```

```python
import concourse.bass as bass
from concourse import mybir
from contextlib import ExitStack


def xattn_ffn_kernel(nc, x, ctx, wq, bq, wk, bk, wv, bv, w_router, w_gating, w_gate, w_up, w_down, out):
    fp32, fp32r = mybir.dt.float32, mybir.dt.float32r
    ALU, ACT, AX = mybir.AluOpType, mybir.ActivationFunctionType, mybir.AxisListType

    B, TQ, D = x.shape
    TK = ctx.shape[1]
    E, _, F = w_gate.shape
    P = 128
    DK = D // P
    KT = 3
    KP = TK // KT
    SK = TK + TK % 2
    PAIRS = B // 2
    TP = 2 * TQ
    T = B * TQ
    CH = 4
    TC = T // CH
    BC = B // CH
    HALVES = 2
    FH = F // HALVES
    FT = FH // P
    STEPS = HALVES * CH * FT
    LAG = 2
    HS = 4
    EARLY = 2 * FT
    SCALE = float(D) ** -0.5
    EPS = 1e-5
    TEMP = 0.1
    DMA = 16

    x_v = x.rearrange("b q d -> q b d")
    out_v = out.rearrange("b q d -> q b d")
    ctx_v = ctx.rearrange("(n two) (p t) d -> n p two (t d)", two=2, t=KT)
    gate_v = w_gate.rearrange("e (k p) (h f) -> e h p k f", p=P, h=HALVES)
    up_v = w_up.rearrange("e (k p) (h f) -> e h p k f", p=P, h=HALVES)
    down_v = w_down.rearrange("e (h t p) d -> e h p t d", p=P, h=HALVES)
    cw_dram = nc.dram_tensor("cw_dram", (E, T), fp32).ap()

    es = ExitStack()
    with es:
        def sb(name, shape, dt=fp32):
            return es.enter_context(nc.sbuf_tensor(name, shape, dt))

        def sem(name):
            return es.enter_context(nc.semaphore(name))

        def at_least(engine, semaphore, count):
            if not isinstance(count, int) or count > 0:
                engine.wait_ge(semaphore, count)

        ident = sb("ident", [P, P])
        ones = sb("ones", [P, TQ])
        eps_c = sb("eps_c", [TQ, B])
        power_c = sb("power_c", [TQ, B])
        zero_c = sb("zero_c", [TQ, B])
        b_raw = sb("b_raw", [P, 2, DK])
        b_split = sb("b_split", [P, 2, DK, 2], fp32r)
        bqk_prod = sb("bqk_prod", [P, DK])
        qbias = sb("qbias", [P, DK])
        vb_sum = sb("vb_sum", [P, DK])
        v_row = sb("v_row", [TQ, D])
        bk_cols = sb("bk_cols", [P, DK, 2, TQ], fp32r)
        c0 = sb("c0", [TQ, 1])
        m_hi = sb("m_hi", [P, DK, D], fp32r)
        m_lo = sb("m_lo", [P, DK, D], fp32r)
        wv_hi = sb("wv_hi", [P, DK, D], fp32r)
        wv_lo = sb("wv_lo", [P, DK, D], fp32r)
        wr_raw = sb("wr_raw", [P, DK, 2 * E])
        wr_split = sb("wr_split", [P, DK, 2, 2 * E], fp32r)
        wr_hi, wr_lo = wr_split[:, :, 0, :], wr_split[:, :, 1, :]
        xs = sb("xs", [TQ, B, D])
        h_in_hi = sb("h_in_hi", [P, DK, T], fp32r)
        h_in_lo = sb("h_in_lo", [P, DK, T], fp32r)
        w_raw = sb("w_raw", [P, 3, DK * FH])
        w_hi = sb("w_hi", [P, HALVES, 3, DK * FH], fp32r)
        w_lo = sb("w_lo", [P, HALVES, 3, DK * FH], fp32r)
        cn_hi, cn_lo = [w[0:KP, HALVES - 1, :, :].rearrange("p a n -> p (a n)")[:, 0:4 * KT * D]
                        .rearrange("p (s b t d) -> p s b t d", s=2, b=2, t=KT) for w in (w_hi, w_lo)]
        ct_hi = sb("ct_hi", [P, 2, DK, SK], fp32r)
        ct_lo = sb("ct_lo", [P, 2, DK, SK], fp32r)
        shared = sb("shared", [P, 4 * KT * D])
        ctx_raw = shared[0:KP, :].rearrange("p (s b n) -> p s b n", s=2, b=2)
        xt_hi = sb("xt_hi", [P, DK, TP], fp32r)
        xt_lo = sb("xt_lo", [P, DK, TP], fp32r)
        q_hi = sb("q_hi", [P, DK, TP], fp32r)
        q_lo = sb("q_lo", [P, DK, TP], fp32r)
        at_hi = sb("at_hi", [P, DK, TP], fp32r)
        at_lo = sb("at_lo", [P, DK, TP], fp32r)
        pt_hi = sb("pt_hi", [KP, 2, KT, TQ], fp32r)
        pt_lo = sb("pt_lo", [KP, 2, KT, TQ], fp32r)
        st_hi = sb("st_hi", [P, DK, TP], fp32r)
        st_lo = sb("st_lo", [P, DK, TP], fp32r)
        bn1 = sb("bn1", [TQ, B, 6])
        mv1 = sb("mv1", [TQ, B, 2])
        bn2 = sb("bn2", [TQ, 2, 6])
        mv2 = sb("mv2", [TQ, 2, 2])
        var1, rstd1, shift1, bias1 = (sb(n, [TQ, B]) for n in ("var1", "rstd1", "shift1", "bias1"))
        var2, rstd2, shift2, bias2 = (sb(n, [TQ, 2]) for n in ("var2", "rstd2", "shift2", "bias2"))
        q_bk = sb("q_bk", [TQ, 2])
        top = sb("top", [TQ, 2])
        top_all = sb("top_all", [TQ, 2])
        neg_top = sb("neg_top", [TQ, 2])
        mass = sb("mass", [TQ, 2])
        inv_mass = sb("inv_mass", [TQ, 2])
        logits = sb("logits", [TQ, B, 2 * E])
        lg = sb("lg", [TQ, B * 2, E])
        lg_f = lg[:, :, :].rearrange("p b e -> p (b e)")
        lg_top = sb("lg_top", [TQ, B * 2])
        lg_sum = sb("lg_sum", [TQ, B * 2])
        cw = sb("cw", [TQ, B, E])
        cw_sum = sb("cw_sum", [TQ, B])
        cw_t = sb("cw_t", [TQ, E, B])
        cw_rows = sb("cw_rows", [P, TQ])
        cw_all = shared[:, 0:T]
        acc = sb("acc", [P, DK, T])
        acc_f = acc[:, :, :].rearrange("p k t -> p (k t)")
        xn = acc_f[0:TQ, 0:2 * D].rearrange("p (b n) -> p b n", b=2)
        at0 = 2 * D
        probs = acc_f[0:TQ, at0:at0 + 2 * TK].rearrange("p (b n) -> p b n", b=2)
        at0 += 2 * TK
        mix = acc_f[0:TQ, at0:at0 + 2 * D].rearrange("p (b n) -> p b n", b=2)
        part = sb("part", [P, 2, DK, TC])
        part_f = part[:, :, :, :].rearrange("p s k t -> p (s k t)")
        q_prod = part_f[0:TQ, 5 * D:7 * D].rearrange("p (b n) -> p b n", b=2)
        xn2 = part_f[0:TQ, 0:2 * D].rearrange("p (b n) -> p b n", b=2)
        bv_all = part_f[0:TQ, 2 * D:3 * D]
        hs = sb("hs", [P, 2, HS, TC], fp32r)
        hs_f = hs[:, :, :, :].rearrange("p a s t -> p (a s t)")
        wt = [hs_f[:, i * DK * D:(i + 1) * DK * D].rearrange("p (k n) -> p k n", k=DK) for i in range(4)]
        wqt_hi, wqt_lo, wkt_hi, wkt_lo = wt
        act = sb("act", [P, 2, TC])
        hid = sb("hid", [P, 2, TC])
        wqk_raw = [w.rearrange("p s t -> p (s t)")[:, 0:DK * D].rearrange("p (k n) -> p k n", k=DK) for w in (act[:, :, :], hid[:, :, :])]
        wv_raw = part_f[:, 3 * D:(3 + DK) * D].rearrange("p (k n) -> p k n", k=DK)

        ps = es.enter_context(nc.psum_tensor("ps", [P, 8, 512], fp32))
        ps_x = ps[:, 0, 0:DK * TP].rearrange("p (k t) -> p k t", k=DK)
        ps_c = ps[:, 1:3, 0:TK]
        ps_s = [ps[0:TQ, 3 + b, 0:SK] for b in range(2)]
        ps_p = [ps[0:KP, 5 + b, 0:KT * TQ].rearrange("p (t q) -> p t q", t=KT) for b in range(2)]
        ps_a = ps[0:TQ, 6, :].rearrange("p (b n) -> p b n", b=2)
        ps_at = ps[:, 6, 0:DK * TP].rearrange("p (k t) -> p k t", k=DK)
        ps_o = ps[0:TQ, 6, :].rearrange("p (b n) -> p b n", b=2)
        ps_x2 = ps[:, 7, 0:DK * TP].rearrange("p (k t) -> p k t", k=DK)
        ps_l = ps[0:TQ, 7, DK * TP:DK * TP + 8 * E].rearrange("p (b s n) -> p b s n", b=2, s=2)
        ps_wt = [ps[:, 5 + i, :].rearrange("p (k n) -> p k n", k=DK) for i in range(2)]
        ps_idle = ps[0:TQ, 7, 0:2 * E * B]
        ps_m = ps[:, 3, :].rearrange("p (k n) -> p k n", k=DK)
        ps_v = ps[0:TQ, 4, 0:D]
        ps_b = ps[:, 4, D:D + 2 * DK].rearrange("p (a two) -> p a two", two=2)
        ps_c0 = ps[0:TQ, 4, D + 2 * DK:D + 2 * DK + 1]
        ps_g = [ps[:, i, 0:TC] for i in range(2)]
        ps_u = [ps[:, 2 + i, 0:TC] for i in range(2)]
        ps_d = [ps[:, 4 + 2 * i:6 + 2 * i, 0:TC] for i in range(2)]
        ps_cw = ps[:, 0, 0:TQ]
        ps_y = [ps[0:TQ, 4 + 2 * i:6 + 2 * i, :] for i in range(2)]

        x_parts = [sem(f"x_part{i}") for i in range(4)]
        weights_in, biases_in, router_in = [sem("wq_in"), sem("wk_in")], sem("biases_in"), sem("router_in")
        wv_in, bv_in = sem("wv_in"), sem("bv_in")
        zeros_set, consts_set, lg_cleared = sem("zeros_set"), sem("consts_set"), sem("lg_cleared")
        wt_ready, wt_hi_done, wt_lo_done = sem("wt_ready"), sem("wt_hi_done"), sem("wt_lo_done")
        m_ready, m_hi_done, m_lo_done = sem("m_ready"), sem("m_hi_done"), sem("m_lo_done")
        b_hi_done, b_split_done, vb_ready, vb_summed, vb_done, q_bk_done = (
            sem(n) for n in ("b_hi_done", "b_split_done", "vb_ready", "vb_summed", "vb_done", "q_bk_done"))
        wv_hi_done, wv_lo_done = sem("wv_hi_done"), sem("wv_lo_done")
        xt_ready, ct_ready, q_ready = sem("xt_ready"), sem("ct_ready"), sem("q_ready")
        scores_ready, pt_ready, mix_ready = sem("scores_ready"), sem("pt_ready"), sem("mix_ready")
        at_ready, o_ready, x2t_ready, logits_ready = sem("at_ready"), sem("o_ready"), sem("x2t_ready"), sem("logits_ready")
        xt_hi_done, ct_hi_done, q_hi_done, probs_done = sem("xt_hi_done"), sem("ct_hi_done"), sem("q_hi_done"), sem("probs_done")
        pt_hi_done, mix_done, at_hi_done, st_hi_done = sem("pt_hi_done"), sem("mix_done"), sem("at_hi_done"), sem("st_hi_done")
        xt_lo_done, ct_lo_done, q_lo_done, pt_lo_done = sem("xt_lo_done"), sem("ct_lo_done"), sem("q_lo_done"), sem("pt_lo_done")
        at_lo_done, st_lo_done = sem("at_lo_done"), sem("st_lo_done")
        stats1_done, xn_done = sem("stats1_done"), sem("xn_done")
        stats2_done, xn2_done = sem("stats2_done"), sem("xn2_done")
        top_done, top_all_done, neg_top_done, mass_inverted = sem("top_done"), sem("top_all_done"), sem("neg_top_done"), sem("mass_inverted")
        x1_done, logits_done = sem("x1_done"), sem("logits_done")
        norm_step, bias1_done, bias2_done = sem("norm_step"), sem("bias1_done"), sem("bias2_done")
        bv_added, cn_hi_done, cn_lo_done = sem("bv_added"), sem("cn_hi_done"), sem("cn_lo_done")
        ctx_in, h_in_done = sem("ctx_in"), sem("h_in_done")
        cw_step, lg_exp, cw_ready, cw_rows_ready, cw_rows_done, cw_stored = (
            sem(n) for n in ("cw_step", "lg_exp", "cw_ready", "cw_rows_ready", "cw_rows_done", "cw_stored"))
        cw_in = [sem(f"cw_in{c}") for c in range(CH)]
        w_in, w_hi_begun, w_hi_done, w_done = sem("w_in"), sem("w_hi_begun"), sem("w_hi_done"), sem("w_done")
        gate_ready, up_ready, down_ready = sem("gate_ready"), sem("up_ready"), sem("down_ready")
        act_done, hid_done, hid_hi_done, hid_lo_done = sem("act_done"), sem("hid_done"), sem("hid_hi_done"), sem("hid_lo_done")
        part_done, acc_done = sem("part_done"), sem("acc_done")
        y_ready, y_done, end_ready, end_done, stored = (sem(n) for n in ("y_ready", "y_done", "end_ready", "end_done", "stored"))

        def inside(p):
            return not isinstance(p, int) or 0 <= p < PAIRS

        def second(p):
            return isinstance(p, int) and p == 1

        def three(w_high, w_low, m_high, m_low):
            return [(w_high, m_high), (w_high, m_low), (w_low, m_high)]

        def accumulate(dst, passes, first=True, last=True):
            for i, (w, m) in enumerate(passes):
                ins = nc.tensor.matmul(dst, w, m, start=first and i == 0, stop=last and i == len(passes) - 1)
            return ins

        def low(dst, src, high):
            return nc.vector.tensor_tensor(dst, src, high.bitcast(fp32), ALU.subtract)

        def half_weights(parts, half):
            gate = parts[:, half, 0, :].rearrange("p (k f) -> p k f", k=DK)
            up = parts[:, half, 1, :].rearrange("p (k f) -> p k f", k=DK)
            down = parts[:, half, 2, :].rearrange("p (t d) -> p t d", t=FT)
            return gate, up, down

        pieces = [(i, slice(j * 512, (j + 1) * 512)) for i in range(3) for j in range(DK * FH // 512)]

        block = es.enter_context(nc.Block())

        @block.sync
        def _(sp):
            for i, src in enumerate((wq, wk)):
                sp.dma_start(wqk_raw[i], src.rearrange("(k p) n -> p k n", p=P)).then_inc(weights_in[i], DMA)
            sp.dma_start(xs[:, 0:2, :], x_v[:, 0:2, :]).then_inc(x_parts[0], DMA)
            with nc.allow_non_contiguous_dma("a few short rows"):
                for i, src in enumerate((bq, bk)):
                    sp.dma_start(b_raw[:, i, :], src.rearrange("(k p) -> p k", p=P)).then_inc(biases_in, DMA)
            sp.dma_start(ctx_raw[:, 0], ctx_v[0]).then_inc(ctx_in, DMA)
            sp.dma_start(xs[:, 2:4, :], x_v[:, 2:4, :]).then_inc(x_parts[1], DMA)
            sp.dma_start(bv_all, bv[None, :].broadcast_to((TQ, D))).then_inc(bv_in, DMA)
            sp.dma_start(wv_raw, wv.rearrange("(k p) n -> p k n", p=P)).then_inc(wv_in, DMA)
            with nc.allow_non_contiguous_dma("a few short rows"):
                for i, src in enumerate((w_router, w_gating)):
                    sp.dma_start(wr_raw[:, :, i * E:(i + 1) * E], src.rearrange("(k p) n -> p k n", p=P)).then_inc(router_in, DMA)
            sp.dma_start(xs[:, 4:8, :], x_v[:, 4:8, :]).then_inc(x_parts[2], DMA)

            def load_ctx(p):
                sp.wait_ge(ctx_in, DMA * p)
                at_least(sp, ct_ready, 2 * (p - 1))
                at_least(sp, cn_lo_done, 2 * (p - 1))
                sp.dma_start(ctx_raw[:, bass.ds(p % 2, 1)], ctx_v[p].rearrange("p (s b) n -> p s b n", s=1)).then_inc(ctx_in, DMA)

            def keep_input(p):
                sp.wait_ge(st_hi_done, p + 1)
                sp.wait_ge(st_lo_done, p + 1)
                sp.dma_start(h_in_hi[:, :, bass.ds(p * TP, TP)].bitcast(fp32), st_hi[:, :, :].bitcast(fp32)).then_inc(h_in_done, DMA)
                sp.dma_start(h_in_lo[:, :, bass.ds(p * TP, TP)].bitcast(fp32), st_lo[:, :, :].bitcast(fp32)).then_inc(h_in_done, DMA)

            def load_weights(e, half):
                at_least(sp, w_done, 2 * e + half)
                for i, v in enumerate((gate_v, up_v)):
                    sp.dma_start(w_raw[:, i, :].rearrange("p (k f) -> p k f", k=DK), v[e, half]).then_inc(w_in, DMA)
                sp.dma_start(w_raw[:, 2, :].rearrange("p (t d) -> p t d", t=FT), down_v[e, half]).then_inc(w_in, DMA)

            def load_cw(e, c):
                sp.dma_start(cw_all[:, c * TC:(c + 1) * TC],
                             cw_dram[e, c * TC:(c + 1) * TC][None, :].broadcast_to((P, TC))).then_inc(cw_in[c], DMA)

            load_ctx(1)
            sp.dma_start(xs[:, 8:B, :], x_v[:, 8:B, :]).then_inc(x_parts[3], DMA)
            load_weights(0, 0)
            load_ctx(2)
            load_ctx(3)
            with sp.Fori(2, PAIRS - 2) as p:
                load_ctx(p + 2)
                keep_input(p - 2)
            load_weights(0, 1)
            for p in range(PAIRS - 4, PAIRS):
                keep_input(p)
            sp.wait_ge(cw_rows_done, 1)
            sp.dma_start(cw_dram.rearrange("e (b t) -> (e b) t", t=TQ), cw_rows[:, :]).then_inc(cw_stored, DMA)
            sp.wait_ge(cw_stored, DMA)
            for c in range(CH):
                load_cw(0, c)
            with sp.Fori(0, E - 1) as e:
                load_weights(e + 1, 0)
                load_weights(e + 1, 1)
                for c in range(CH):
                    sp.wait_ge(part_done, 2 * CH * e + CH + c + 1)
                    load_cw(e + 1, c)
            for c in range(CH - 1):
                sp.wait_ge(y_done, c + 2)
                sp.dma_start(out_v[:, c * BC:(c + 1) * BC, :], xs[:, c * BC:(c + 1) * BC, :]).then_inc(stored, DMA)
            for j in range(2):
                sp.wait_ge(end_done, j + 1)
                bs = slice(B - BC + j * BC // 2, B - BC + (j + 1) * BC // 2)
                sp.dma_start(out_v[:, bs, :], xs[:, bs, :]).then_inc(stored, DMA)
            sp.wait_ge(stored, DMA * (CH + 1))

        @block.gpsimd
        def _(pool):
            nc.gpsimd.memset(ident[:], 0.0).then_inc(zeros_set, 1)
            nc.gpsimd.memset(eps_c[:], EPS)
            nc.gpsimd.memset(power_c[:], -0.5)
            nc.gpsimd.memset(zero_c[:], 0.0)
            nc.gpsimd.memset(ones[:], 1.0)
            if SK > TK:
                for t in (ct_hi, ct_lo):
                    nc.gpsimd.memset(t[:, :, :, TK:SK].bitcast(fp32), 0.0)
            pool.wait_ge(zeros_set, 1)
            nc.gpsimd.affine_select(out=ident[:], in_=ident[:], compare_op=ALU.not_equal, fill=1.0, base=0,
                                    pattern=[[-1, P]], channel_multiplier=1).then_inc(consts_set, 1)
            pool.wait_ge(consts_set, 1)

            def norm_terms(mv, var, root, shift, bias, n, steps, done):
                nc.gpsimd.tensor_tensor(var, mv[:, :, 1], eps_c[:, 0:n], ALU.add).then_inc(norm_step, 1)
                pool.wait_ge(norm_step, steps + 1)
                nc.gpsimd.tensor_tensor(root, var, power_c[:, 0:n], ALU.pow).then_inc(norm_step, 1)
                pool.wait_ge(norm_step, steps + 2)
                nc.gpsimd.tensor_tensor(shift, mv[:, :, 0], root, ALU.mult).then_inc(norm_step, 1)
                pool.wait_ge(norm_step, steps + 3)
                nc.gpsimd.tensor_tensor(bias, zero_c[:, 0:n], shift, ALU.subtract).then_inc(done, 1)

            def norm2_terms(p, steps):
                pool.wait_ge(stats2_done, p + 1)
                norm_terms(mv2[:], var2[:], rstd2[:], shift2[:], bias2[:], 2, steps, bias2_done)

            def low_ctx(p):
                for b in range(2):
                    pool.wait_ge(cn_hi_done, 2 * p + b + 1)
                    nc.gpsimd.tensor_tensor(cn_lo[:, bass.ds(p % 2, 1), b, :, :], ctx_raw[:, bass.ds(p % 2, 1), b, :].rearrange("p s (t d) -> p s t d", t=KT),
                                            cn_hi[:, bass.ds(p % 2, 1), b, :, :].bitcast(fp32), ALU.subtract).then_inc(cn_lo_done, 1)

            def add_bv(p):
                pool.wait_ge(xn_done, p + 1)
                for b in range(2):
                    rows = xs[:, bass.ds(2 * p + b, 1), :]
                    ins = nc.gpsimd.tensor_tensor(rows, rows, bv_all[:, None, :], ALU.add)
                ins.then_inc(bv_added, 1)

            def low_weights(e, half, some=pieces):
                n = 2 * e + half
                pool.wait_ge(w_hi_done if some[-1] == pieces[-1] else w_hi_begun, n + 1)
                for i, s in some:
                    ins = nc.gpsimd.tensor_tensor(w_lo[:, half, i, s], w_raw[:, i, s], w_hi[:, half, i, s].bitcast(fp32), ALU.subtract)
                if some[-1] == pieces[-1]:
                    ins.then_inc(w_done, 1)

            def pair(p):
                if inside(p - 2):
                    norm2_terms(p - 2, 3 * (p + 2))
                if inside(p):
                    low_ctx(p)
                if inside(p + 1):
                    add_bv(p + 1)

            def norm1_terms(before, rows, stats):
                pool.wait_ge(stats1_done, stats)
                norm_terms(mv1[:, rows], var1[:, rows], rstd1[:, rows], shift1[:, rows], bias1[:, rows],
                           rows.stop - rows.start, 3 * before, bias1_done)

            norm1_terms(0, slice(0, 2), 1)
            norm1_terms(1, slice(2, 4), 2)
            low_ctx(0)
            pool.wait_ge(bv_in, DMA)
            add_bv(0)
            add_bv(1)
            norm1_terms(2, slice(4, 8), 3)
            low_ctx(1)
            low_weights(0, 0, pieces[:3])
            add_bv(2)
            low_weights(0, 0, pieces[3:])
            norm2_terms(0, 3 * 3)
            low_ctx(2)
            norm1_terms(4, slice(8, B), 6)
            add_bv(3)
            with pool.Fori(3, PAIRS - 2) as p:
                pair(p)
            for p in range(PAIRS - 2, PAIRS + 2):
                pair(p)

            def add_part(k, c):
                pool.wait_ge(part_done, k + 1)
                at_least(pool, acc_done, k - 2 * CH + 1)
                a = acc[:, :, c * TC:(c + 1) * TC]
                nc.gpsimd.tensor_tensor(a, a, part[:, c % 2, :, :], ALU.add).then_inc(acc_done, 1)

            def expert(e, first=False, last=False):
                if not first:
                    add_part(2 * CH * e - 1, CH - 1)
                low_weights(e, 1)
                if not first:
                    for c in range(CH):
                        add_part(2 * CH * e + c, c)
                if not last:
                    low_weights(e + 1, 0)
                for c in range(CH - 1):
                    add_part(2 * CH * e + CH + c, c)

            expert(0, first=True)
            with pool.Fori(1, E - 1) as e:
                expert(e)
            expert(E - 1, last=True)

        @block.scalar
        def _(sc):
            def norm1(p):
                for b in range(2):
                    i = bass.ds(2 * p + b, 1)
                    ins = nc.scalar.activation(xn[:, b, :], xs[:, i, :], ACT.Identity, bias=bias1[:, i], scale=rstd1[:, i])
                ins.then_inc(xn_done, 1)

            def norm2(p):
                sc.wait_ge(bias2_done, p + 1)
                for b in range(2):
                    ins = nc.scalar.activation(xn2[:, b, :], xs[:, bass.ds(2 * p + b, 1), :], ACT.Identity,
                                               bias=bias2[:, b:b + 1], scale=rstd2[:, b:b + 1])
                ins.then_inc(xn2_done, 1)

            def xt_high(p):
                sc.wait_ge(xt_ready, p + 1)
                nc.scalar.copy(xt_hi[:], ps_x).then_inc(xt_hi_done, 1)

            def ct_high(p, b):
                sc.wait_ge(ct_ready, 2 * p + b + 1)
                nc.scalar.copy(ct_hi[:, b, :, 0:TK], ps_c).then_inc(ct_hi_done, 1)

            def q_high(p):
                sc.wait_ge(q_ready, p + 1)
                for j in range(DK):
                    ins = nc.scalar.activation(q_hi[:, j, :], ps_x[:, j, :], ACT.Identity, bias=qbias[:, j:j + 1])
                ins.then_inc(q_hi_done, 1)

            def exponentials(p, b):
                sc.wait_ge(neg_top_done, p + 1)
                nc.scalar.activation(probs[:, b, :], ps_s[b][:, 0:TK], ACT.Exp, bias=neg_top[:, b:b + 1],
                                     accum_out=mass[:, b:b + 1]).then_inc(probs_done, 1)

            def pt_high(p, b):
                sc.wait_ge(pt_ready, 2 * p + b + 1)
                nc.scalar.copy(pt_hi[:, b, :, :], ps_p[b]).then_inc(pt_hi_done, 1)

            def normalise(p):
                sc.wait_ge(mix_ready, p + 1)
                sc.wait_ge(mass_inverted, p + 1)
                for b in range(2):
                    ins = nc.scalar.activation(mix[:, b, :], ps_a[:, b, :], ACT.Identity, scale=inv_mass[:, b:b + 1])
                ins.then_inc(mix_done, 1)

            def at_high(p):
                sc.wait_ge(at_ready, p + 1)
                nc.scalar.copy(at_hi[:], ps_at).then_inc(at_hi_done, 1)

            def st_high(p):
                sc.wait_ge(x2t_ready, p + 1)
                at_least(sc, h_in_done, 2 * DMA * p)
                nc.scalar.copy(st_hi[:], ps_x2).then_inc(st_hi_done, 1)

            def cn_high(p):
                sc.wait_ge(ctx_in, DMA * (p + 1))
                at_least(sc, mix_ready, p - 1)
                for b in range(2):
                    nc.scalar.copy(cn_hi[:, bass.ds(p % 2, 1), b, :, :],
                                   ctx_raw[:, bass.ds(p % 2, 1), b, :].rearrange("p s (t d) -> p s t d", t=KT)).then_inc(cn_hi_done, 1)

            def high_weights(e, half, some=pieces):
                n = 2 * e + half
                sc.wait_ge(w_in, 3 * DMA * (n + 1))
                at_least(sc, down_ready, CH * (n - 1))
                for i, s in some:
                    ins = nc.scalar.copy(w_hi[:, half, i, s], w_raw[:, i, s])
                ins.then_inc(w_hi_done if some[-1] == pieces[-1] else w_hi_begun, 1)

            def activate(e, s):
                n = STEPS * e + s
                sc.wait_ge(gate_ready, n + 1)
                at_least(sc, hid_done, n - 1)
                nc.scalar.activation(act[:, s % 2, :], ps_g[s % 2], ACT.Silu).then_inc(act_done, 1)
                sc.wait_ge(hid_done, n + 1)
                nc.scalar.copy(hs[:, 0, s % HS, :], hid[:, s % 2, :]).then_inc(hid_hi_done, 1)

            for i, hi in enumerate((wqt_hi, wkt_hi)):
                sc.wait_ge(wt_ready, i + 1)
                nc.scalar.copy(hi, ps_wt[i]).then_inc(wt_hi_done, 1)
            sc.wait_ge(bias1_done, 1)
            norm1(0)
            sc.wait_ge(m_ready, 1)
            nc.scalar.mul(m_hi[:], ps_m, SCALE).then_inc(m_hi_done, 1)
            xt_high(0)
            ct_high(0, 0)
            cn_high(0)
            sc.wait_ge(vb_done, 1)
            q_high(0)
            ct_high(0, 1)
            sc.wait_ge(bias1_done, 2)
            sc.wait_ge(q_bk_done, 1)
            norm1(1)
            ct_high(1, 0)
            sc.wait_ge(wv_in, DMA)
            nc.scalar.copy(wv_hi[:], wv_raw).then_inc(wv_hi_done, 1)
            sc.wait_ge(router_in, 2 * DMA)
            nc.scalar.copy(wr_hi, wr_raw[:]).then_inc(wv_hi_done, 1)

            def pair(p):
                if inside(p - 1):
                    pt_high(p - 1, 0)
                if inside(p + 1):
                    xt_high(p + 1)
                if inside(p - 1):
                    pt_high(p - 1, 1)
                if not inside(p - 1):
                    cn_high(p + 1)
                if inside(p - 2):
                    cn_high(p)
                if second(p):
                    high_weights(0, 0, pieces[:3])
                if inside(p + 1) and inside(p - 1):
                    ct_high(p + 1, 0)
                if second(p):
                    high_weights(0, 0, pieces[3:])
                if inside(p - 2):
                    norm2(p - 2)
                if inside(p - 1):
                    normalise(p - 1)
                if inside(p + 1):
                    ct_high(p + 1, 1)
                else:
                    exponentials(p, 0)
                    exponentials(p, 1)
                if inside(p - 1):
                    at_high(p - 1)
                if inside(p - 2):
                    st_high(p - 2)
                if inside(p + 1):
                    exponentials(p, 0)
                    q_high(p + 1)
                    exponentials(p, 1)
                else:
                    activate(0, 0)
                    activate(0, 1)
                if inside(p + 2):
                    sc.wait_ge(bias1_done, 4 if inside(p - 2) else 3)
                    sc.wait_ge(q_bk_done, p + 2)
                    norm1(p + 2)

            pair(0)
            pair(1)
            with sc.Fori(2, PAIRS - 2) as p:
                pair(p)
            for p in range(PAIRS - 2, PAIRS):
                pair(p)
            last_pair = PAIRS - 1
            pt_high(last_pair, 0)
            pt_high(last_pair, 1)
            activate(0, 2)
            normalise(last_pair)
            at_high(last_pair)
            norm2(last_pair - 1)
            activate(0, 3)
            st_high(last_pair - 1)
            activate(0, 4)
            norm2(last_pair)
            st_high(last_pair)
            activate(0, 5)
            sc.wait_ge(cw_step, 2)
            lgv = lg[:, :, :].rearrange("p (b two) e -> p b two e", two=2)
            nc.scalar.activation(lgv[:, :, 0, :], lgv[:, :, 0, :], ACT.Exp)
            nc.scalar.activation(lgv[:, :, 1, :], lgv[:, :, 1, :], ACT.Exp, scale=1.0 / TEMP).then_inc(lg_exp, 1)
            activate(0, 6)
            activate(0, 7)

            def expert(e, first=False, last=False):
                for s in range(EARLY if first else 0, STEPS):
                    if s == (EARLY if first else LAG):
                        high_weights(e, 1)
                    if s == STEPS // 2 + LAG and not last:
                        high_weights(e + 1, 0)
                    activate(e, s)

            expert(0, first=True)
            with sc.Fori(1, E - 1) as e:
                expert(e)
            expert(E - 1, last=True)

        @block.vector
        def _(ve):
            def stats1(first, end):
                for b in range(first, end):
                    nc.vector.bn_stats(bn1[:, b, :], xs[:, b, :])
                nc.vector.drain()
                for b in range(first, end):
                    ins = nc.vector.bn_aggr(mv1[:, b, :], bn1[:, b, :])
                ins.then_inc(stats1_done, 1)

            def xt_low(p):
                ve.wait_ge(xt_hi_done, p + 1)
                low(xt_lo[:], ps_x, xt_hi[:]).then_inc(xt_lo_done, 1)

            def ct_low(p, b):
                ve.wait_ge(ct_hi_done, 2 * p + b + 1)
                low(ct_lo[:, b, :, 0:TK], ps_c, ct_hi[:, b, :, 0:TK]).then_inc(ct_lo_done, 1)

            def q_low(p):
                ve.wait_ge(q_hi_done, p + 1)
                for j in range(DK):
                    ins = nc.vector.scalar_tensor_tensor(q_lo[:, j, :], ps_x[:, j, :], qbias[:, j:j + 1],
                                                         q_hi[:, j, :].bitcast(fp32), ALU.add, ALU.subtract)
                ins.then_inc(q_lo_done, 1)

            def times_bk(p):
                nc.vector.drain()
                for b in range(2):
                    ins = nc.vector.tensor_tensor_reduce(q_prod[:, b, :], xn[:, b, :], v_row[:], 1.0, 0.0, ALU.mult, ALU.add,
                                                         accum_out=q_bk[:, b:b + 1])
                ins.then_inc(q_bk_done, 1)

            def maxima(p):
                for b in range(2):
                    ve.wait_ge(scores_ready, 2 * p + b + 1)
                    ins = nc.vector.tensor_reduce(top[:, b:b + 1], ps_s[b][:, 0:TK], AX.X, ALU.max)
                ins.then_inc(top_done, 1)
                ve.wait_ge(q_bk_done, p + 1)
                ve.wait_ge(top_done, p + 1)
                nc.vector.scalar_tensor_tensor(top_all[:], q_bk[:], c0[:, 0:1], top[:], ALU.add, ALU.add).then_inc(top_all_done, 1)
                ve.wait_ge(top_all_done, p + 1)
                nc.vector.scalar_tensor_tensor(neg_top[:], q_bk[:], c0[:, 0:1], top_all[:], ALU.add, ALU.subtract).then_inc(neg_top_done, 1)

            def pt_low(p, b):
                ve.wait_ge(pt_hi_done, 2 * p + b + 1)
                low(pt_lo[:, b, :, :], ps_p[b], pt_hi[:, b, :, :]).then_inc(pt_lo_done, 1)

            def invert_mass(p):
                ve.wait_ge(probs_done, 2 * p + 2)
                nc.vector.reciprocal(inv_mass[:], mass[:]).then_inc(mass_inverted, 1)

            def at_low(p):
                ve.wait_ge(at_hi_done, p + 1)
                low(at_lo[:], ps_at, at_hi[:]).then_inc(at_lo_done, 1)

            def st_low(p):
                ve.wait_ge(st_hi_done, p + 1)
                low(st_lo[:], ps_x2, st_hi[:]).then_inc(st_lo_done, 1)

            def residual1(p):
                ve.wait_ge(o_ready, p + 1)
                ve.wait_ge(bv_added, p + 1)
                rows = xs[:, bass.ds(2 * p, 2), :]
                nc.vector.tensor_tensor(rows, rows, ps_o, ALU.add).then_inc(x1_done, 1)

            def stats2(p):
                nc.vector.drain()
                for b in range(2):
                    ins = nc.vector.bn_stats(bn2[:, b, :], xs[:, bass.ds(2 * p + b, 1), :])
                nc.vector.drain()
                for b in range(2):
                    ins = nc.vector.bn_aggr(mv2[:, b, :], bn2[:, b, :])
                ins.then_inc(stats2_done, 1)

            def keep_logits(p):
                ve.wait_ge(logits_ready, p + 1)
                nc.vector.tensor_reduce(logits[:, bass.ds(2 * p, 2), :], ps_l.rearrange("p b s n -> p b n s"), AX.X, ALU.add).then_inc(logits_done, 1)

            def hidden(e, s):
                n = STEPS * e + s
                ve.wait_ge(act_done, n + 1)
                ve.wait_ge(up_ready, n + 1)
                at_least(ve, hid_hi_done, n - 1)
                nc.vector.tensor_tensor(hid[:, s % 2, :], act[:, s % 2, :], ps_u[s % 2], ALU.mult).then_inc(hid_done, 1)
                ve.wait_ge(hid_hi_done, n + 1)
                low(hs[:, 1, s % HS, :], hid[:, s % 2, :], hs[:, 0, s % HS, :]).then_inc(hid_lo_done, 1)

            nc.vector.memset(lg_f, 0.0).then_inc(lg_cleared, 1)
            ve.wait_ge(x_parts[0], DMA)
            stats1(0, 2)
            ve.wait_ge(biases_in, 2 * DMA)
            nc.vector.tensor_copy(b_split[:, :, :, 0], b_raw[:])
            nc.vector.tensor_tensor(bqk_prod[:], b_raw[:, 0, :], b_raw[:, 1, :], ALU.mult).then_inc(b_hi_done, 1)
            ve.wait_ge(b_hi_done, 1)
            low(b_split[:, :, :, 1], b_raw[:], b_split[:, :, :, 0]).then_inc(b_hi_done, 1)
            for i, (hi, lo) in enumerate(((wqt_hi, wqt_lo), (wkt_hi, wkt_lo))):
                ve.wait_ge(wt_hi_done, i + 1)
                low(lo, ps_wt[i], hi).then_inc(wt_lo_done, 1)
            ve.wait_ge(b_hi_done, 2)
            nc.vector.tensor_copy(bk_cols[:, :, :, :], b_split[:, 1, :, :, None].bitcast(fp32).broadcast_to((P, DK, 2, TQ))).then_inc(b_split_done, 1)
            ve.wait_ge(x_parts[1], DMA)
            stats1(2, 4)
            ve.wait_ge(m_hi_done, 1)
            nc.vector.scalar_tensor_tensor(m_lo[:], ps_m, SCALE, m_hi[:].bitcast(fp32), ALU.mult, ALU.subtract).then_inc(m_lo_done, 1)
            xt_low(0)
            ct_low(0, 0)
            ve.wait_ge(vb_ready, 1)
            nc.vector.tensor_reduce(vb_sum[:], ps_b, AX.X, ALU.add).then_inc(vb_summed, 1)
            nc.vector.tensor_scalar(v_row[:], ps_v, SCALE, None, ALU.mult).then_inc(vb_summed, 1)
            nc.vector.tensor_scalar(c0[:], ps_c0, SCALE, None, ALU.mult)
            ve.wait_ge(vb_summed, 2)
            nc.vector.tensor_scalar(qbias[:], vb_sum[:], SCALE, None, ALU.mult).then_inc(vb_done, 1)
            times_bk(0)
            q_low(0)
            ct_low(0, 1)
            ve.wait_ge(x_parts[2], DMA)
            stats1(4, 8)
            ct_low(1, 0)

            def pair(p):
                if inside(p - 1):
                    invert_mass(p - 1)
                    pt_low(p - 1, 0)
                if second(p):
                    ve.wait_ge(wv_hi_done, 2)
                    low(wv_lo[:], wv_raw, wv_hi[:]).then_inc(wv_lo_done, 1)
                    low(wr_lo, wr_raw[:], wr_hi).then_inc(wv_lo_done, 1)
                if inside(p - 1):
                    pt_low(p - 1, 1)
                if inside(p + 1):
                    xt_low(p + 1)
                if second(p):
                    ve.wait_ge(x_parts[3], DMA)
                    stats1(8, 12)
                if inside(p + 1) and inside(p - 1):
                    ct_low(p + 1, 0)
                maxima(p)
                if inside(p + 1):
                    times_bk(p + 1)
                if second(p):
                    stats1(12, 14)
                if inside(p - 1):
                    at_low(p - 1)
                if inside(p - 2):
                    st_low(p - 2)
                if inside(p + 1):
                    ct_low(p + 1, 1)
                else:
                    hidden(0, 0)
                    hidden(0, 1)
                if inside(p + 1):
                    q_low(p + 1)
                if inside(p - 1):
                    residual1(p - 1)
                if inside(p - 1) and inside(p + 1):
                    stats2(p - 1)
                if second(p):
                    stats1(14, B)
                if inside(p - 2):
                    keep_logits(p - 2)

            pair(0)
            pair(1)
            with ve.Fori(1, PAIRS // 2 - 1) as n:
                pair(2 * n)
                pair(2 * n + 1)
            for p in range(PAIRS - 2, PAIRS):
                pair(p)
            last_pair = PAIRS - 1
            invert_mass(last_pair)
            pt_low(last_pair, 0)
            pt_low(last_pair, 1)
            hidden(0, 2)
            stats2(last_pair - 1)
            at_low(last_pair)
            hidden(0, 3)
            ve.wait_ge(xn2_done, last_pair)
            residual1(last_pair)
            stats2(last_pair)
            st_low(last_pair - 1)
            hidden(0, 4)
            keep_logits(last_pair - 1)
            st_low(last_pair)
            hidden(0, 5)
            keep_logits(last_pair)
            lv = logits[:, :, :].rearrange("p b (two e) -> p (b two) e", two=2)
            ve.wait_ge(logits_done, PAIRS)
            nc.vector.tensor_reduce(lg_top[:], lv, AX.X, ALU.max).then_inc(cw_step, 1)
            ve.wait_ge(cw_step, 1)
            nc.vector.tensor_tensor(lg[:], lv, lg_top[:, :, None].broadcast_to((TQ, 2 * B, E)), ALU.subtract).then_inc(cw_step, 1)
            ve.wait_ge(lg_exp, 1)
            nc.vector.tensor_reduce(lg_sum[:], lg[:], AX.X, ALU.add).then_inc(cw_step, 1)
            ve.wait_ge(cw_step, 3)
            nc.vector.reciprocal(lg_top[:], lg_sum[:]).then_inc(cw_step, 1)
            ve.wait_ge(cw_step, 4)
            nc.vector.tensor_tensor(lg[:], lg[:], lg_top[:, :, None].broadcast_to((TQ, 2 * B, E)), ALU.mult).then_inc(cw_step, 1)
            ve.wait_ge(cw_step, 5)
            lgv = lg[:, :, :].rearrange("p (b two) e -> p b two e", two=2)
            nc.vector.tensor_tensor(cw[:], lgv[:, :, 0, :], lgv[:, :, 1, :], ALU.mult).then_inc(cw_step, 1)
            ve.wait_ge(cw_step, 6)
            nc.vector.tensor_reduce(cw_sum[:], cw[:], AX.X, ALU.add).then_inc(cw_step, 1)
            ve.wait_ge(cw_step, 7)
            nc.vector.tensor_scalar(cw_sum[:], cw_sum[:], 1e-9, None, ALU.add).then_inc(cw_step, 1)
            ve.wait_ge(cw_step, 8)
            nc.vector.reciprocal(lg_sum[:, 0:B], cw_sum[:]).then_inc(cw_step, 1)
            ve.wait_ge(cw_step, 9)
            nc.vector.tensor_tensor(cw_t[:, :, :].rearrange("p e b -> p b e"), cw[:],
                                    lg_sum[:, 0:B, None].broadcast_to((TQ, B, E)), ALU.mult).then_inc(cw_ready, 1)
            ve.wait_ge(cw_rows_ready, 1)
            nc.vector.tensor_copy(cw_rows[:], ps_cw).then_inc(cw_rows_done, 1)
            hidden(0, 6)
            hidden(0, 7)

            def expert(e, first=False, last=False):
                for s in range(EARLY if first else 0, STEPS + (LAG if last else 0)):
                    if s < STEPS:
                        hidden(e, s)
                    turn = 2 * FT if first and s == 2 * FT else s - 1 if s % FT == 1 and not (first and s in (1, FT + 1)) else None
                    if turn is not None and not (last and s > STEPS):
                        i = 0 if s == 2 * FT else turn // FT - 1
                        k, c = 2 * CH * e + i, i % CH
                        ve.wait_ge(down_ready, k + 1)
                        ve.wait_ge(cw_in[c], DMA * ((e if i >= 0 else e - 1) + 1))
                        fresh = first and 0 <= i < CH
                        if not fresh:
                            at_least(ve, acc_done, k - 2 - CH + 1)
                        dst = acc[:, :, c * TC:(c + 1) * TC] if fresh else part[:, c % 2, :, :]
                        nc.vector.tensor_tensor(dst, ps_d[c % 2], cw_all[:, None, c * TC:(c + 1) * TC].broadcast_to((P, DK, TC)),
                                                ALU.mult).then_inc(part_done, 1)
                    if last and s > STEPS // 2 and s % FT == 0:
                        residual2((s - STEPS // 2) // FT - 1)

            def residual2(n):
                c = (n - 1) % CH
                ve.wait_ge(y_ready, n + 1)
                rows = xs[:, c * BC:(c + 1) * BC, :].rearrange("p (k b) d -> p k (b d)", k=DK)
                nc.vector.tensor_tensor(rows, rows, ps_y[c % 2], ALU.add).then_inc(y_done, 1)

            def residual_end(j):
                ve.wait_ge(end_ready, j + 1)
                for i in range(BC // 2):
                    b = B - BC + j * BC // 2 + i
                    ins = nc.vector.scalar_tensor_tensor(xs[:, b, :], ps_y[1][:, j, i * D:(i + 1) * D], cw_t[:, E - 1, b:b + 1],
                                                         xs[:, b, :], ALU.mult, ALU.add)
                ins.then_inc(end_done, 1)

            expert(0, first=True)
            with ve.Fori(1, E - 1) as e:
                expert(e)
            expert(E - 1, last=True)
            ve.wait_ge(y_done, CH)
            for j in range(2):
                residual_end(j)

        @block.tensor
        def _(pe):
            def transpose_norm(p):
                pe.wait_ge(xn_done, p + 1)
                at_least(pe, q_lo_done, p)
                for b in range(2):
                    for k in range(DK):
                        ins = nc.tensor.transpose(ps_x[:, k, b * TQ:(b + 1) * TQ], xn[:, b, k * P:(k + 1) * P], ident[0:TQ, 0:TQ])
                ins.then_inc(xt_ready, 1)

            def transpose_ctx(p, b, slot):
                pe.wait_ge(ctx_in, DMA * (p + 1))
                at_least(pe, ct_lo_done, 2 * p + b)
                for k in range(DK):
                    for t in range(KT):
                        at = t * D + k * P
                        ins = nc.tensor.transpose(ps_c[:, k, t * KP:(t + 1) * KP], ctx_raw[:, slot, b, at:at + P], ident[0:KP, 0:KP])
                ins.then_inc(ct_ready, 1)

            def queries(p):
                pe.wait_ge(xt_lo_done, p + 1)
                for j in range(DK):
                    cols = slice(j * P, (j + 1) * P)
                    ins = accumulate(ps_x[:, j, :], [t for k in range(DK) for t in
                                                     three(m_hi[:, k, cols], m_lo[:, k, cols], xt_hi[:, k, :], xt_lo[:, k, :])])
                ins.then_inc(q_ready, 1)

            def scores(p, b):
                if b == 0:
                    pe.wait_ge(q_lo_done, p + 1)
                pe.wait_ge(ct_lo_done, 2 * p + b + 1)
                rows = slice(b * TQ, (b + 1) * TQ)
                accumulate(ps_s[b], [t for k in range(DK) for t in
                                     three(q_hi[:, k, rows], q_lo[:, k, rows], ct_hi[:, b, k, :], ct_lo[:, b, k, :])]).then_inc(scores_ready, 1)

            def transpose_probs(p, b):
                pe.wait_ge(probs_done, 2 * p + b + 1)
                if b == 1:
                    at_least(pe, x1_done, p)
                for t in range(KT):
                    ins = nc.tensor.transpose(ps_p[b][:, t, :], probs[:, b, t * KP:(t + 1) * KP], ident[0:TQ, 0:TQ])
                ins.then_inc(pt_ready, 1)

            def mix_ctx(p):
                pe.wait_ge(pt_lo_done, 2 * p + 2)
                pe.wait_ge(cn_lo_done, 2 * p + 2)
                for b in range(2):
                    ins = accumulate(ps_a[:, b, :], [x for t in range(KT) for x in
                                                     three(pt_hi[:, b, t, :], pt_lo[:, b, t, :], cn_hi[:, p % 2, b, t, :], cn_lo[:, p % 2, b, t, :])])
                ins.then_inc(mix_ready, 1)

            def transpose_mix(p):
                pe.wait_ge(mix_done, p + 1)
                for b in range(2):
                    for k in range(DK):
                        ins = nc.tensor.transpose(ps_at[:, k, b * TQ:(b + 1) * TQ], mix[:, b, k * P:(k + 1) * P], ident[0:TQ, 0:TQ])
                ins.then_inc(at_ready, 1)

            def values(p):
                pe.wait_ge(at_lo_done, p + 1)
                for b in range(2):
                    rows = slice(b * TQ, (b + 1) * TQ)
                    ins = accumulate(ps_o[:, b, :], [t for k in range(DK) for t in
                                                     three(at_hi[:, k, rows], at_lo[:, k, rows], wv_hi[:, k, :], wv_lo[:, k, :])])
                ins.then_inc(o_ready, 1)

            def transpose_norm2(p):
                pe.wait_ge(xn2_done, p + 1)
                at_least(pe, logits_done, p)
                for b in range(2):
                    for k in range(DK):
                        ins = nc.tensor.transpose(ps_x2[:, k, b * TQ:(b + 1) * TQ], xn2[:, b, k * P:(k + 1) * P], ident[0:TQ, 0:TQ])
                ins.then_inc(x2t_ready, 1)

            def route(p):
                pe.wait_ge(st_lo_done, p + 1)
                for b in range(2):
                    rows = slice(b * TQ, (b + 1) * TQ)
                    for k in range(DK):
                        nc.tensor.matmul(ps_l[:, b, :, :].rearrange("p s n -> p (s n)"), st_hi[:, k, rows],
                                         wr_split[:, k, :, :].rearrange("p s n -> p (s n)"), start=k == 0, stop=False)
                        ins = nc.tensor.matmul(ps_l[:, b, 0, :], st_lo[:, k, rows], wr_hi[:, k, :], start=False, stop=k == DK - 1)
                ins.then_inc(logits_ready, 1)

            def keep_busy(n):
                for _ in range(n):
                    nc.tensor.matmul(ps_idle, lg_f[:, 0:TQ], lg_f, start=True, stop=True)

            pe.wait_ge(lg_cleared, 1)
            keep_busy(3)
            pe.wait_ge(consts_set, 1)
            for i in range(2):
                pe.wait_ge(weights_in[i], DMA)
                for et in range(DK):
                    for k in range(DK):
                        ins = nc.tensor.transpose(ps_wt[i][:, et, k * P:(k + 1) * P], wqk_raw[i][:, k, et * P:(et + 1) * P], ident[:])
                ins.then_inc(wt_ready, 1)
            keep_busy(2)
            pe.wait_ge(wt_lo_done, 2)
            for it in range(DK):
                cols = slice(it * P, (it + 1) * P)
                ins = accumulate(ps_m[:, it, :], [t for et in range(DK) for t in
                                                  three(wqt_hi[:, et, cols], wqt_lo[:, et, cols], wkt_hi[:, et, :], wkt_lo[:, et, :])])
            ins.then_inc(m_ready, 1)
            transpose_norm(0)
            transpose_ctx(0, 0, 0)
            pe.wait_ge(b_split_done, 1)
            accumulate(ps_v, [t for et in range(DK) for t in
                              three(bk_cols[:, et, 0, :], bk_cols[:, et, 1, :], wqt_hi[:, et, :], wqt_lo[:, et, :])])
            for j in range(DK):
                cols = slice(j * P, (j + 1) * P)
                accumulate(ps_b[:, j, :], [(w[:, et, cols], b_split[:, 0, et, :]) for et in range(DK) for w in (wkt_hi, wkt_lo)])
            accumulate(ps_c0, [(ones[:], bqk_prod[:, et:et + 1]) for et in range(DK)]).then_inc(vb_ready, 1)
            pe.wait_ge(m_lo_done, 1)
            queries(0)
            transpose_ctx(0, 1, 0)

            def pair(p, slot):
                if inside(p - 1):
                    transpose_probs(p - 1, 0)
                else:
                    scores(p, 0)
                    transpose_ctx(p + 1, 0, 1 - slot)
                if second(p):
                    keep_busy(4)
                if inside(p + 1):
                    transpose_norm(p + 1)
                if inside(p - 1):
                    transpose_probs(p - 1, 1)
                    scores(p, 0)
                else:
                    scores(p, 1)
                if inside(p + 1) and inside(p - 1):
                    transpose_ctx(p + 1, 0, 1 - slot)
                if inside(p - 1):
                    scores(p, 1)
                    mix_ctx(p - 1)
                if not inside(p + 1):
                    gate_up(0, 0, first=True)
                if inside(p + 1):
                    transpose_ctx(p + 1, 1, 1 - slot)
                if inside(p - 2):
                    transpose_norm2(p - 2)
                if inside(p - 1):
                    transpose_mix(p - 1)
                if inside(p + 1):
                    queries(p + 1)
                if not inside(p + 1):
                    pe.wait_ge(probs_done, 2 * PAIRS - 1)
                    gate_up(0, 1)
                if inside(p - 1):
                    if not inside(p - 2):
                        pe.wait_ge(wv_lo_done, 2)
                    values(p - 1)
                if inside(p - 2):
                    route(p - 2)

            def gate_up(e, s, first=False):
                n = STEPS * e + s
                half, c, f = s // (CH * FT), s // FT % CH, s % FT
                gate_hi, up_hi, _ = half_weights(w_hi, half)
                gate_lo, up_lo, _ = half_weights(w_lo, half)
                cols, toks = slice(f * P, (f + 1) * P), slice(c * TC, (c + 1) * TC)
                if s % (CH * FT) == 0:
                    pe.wait_ge(w_done, 2 * e + half + 1)
                if first and half == 0 and f == 0:
                    pe.wait_ge(h_in_done, 2 * DMA * PAIRS // CH * (c + 1))
                if first and s == EARLY:
                    pe.wait_ge(cw_rows_done, 1)
                at_least(pe, act_done, n - 1)
                accumulate(ps_g[s % 2], [t for k in range(DK) for t in
                                         three(gate_hi[:, k, cols], gate_lo[:, k, cols], h_in_hi[:, k, toks], h_in_lo[:, k, toks])]
                           ).then_inc(gate_ready, 1)
                at_least(pe, hid_done, n - 1)
                accumulate(ps_u[s % 2], [t for k in range(DK) for t in
                                         three(up_hi[:, k, cols], up_lo[:, k, cols], h_in_hi[:, k, toks], h_in_lo[:, k, toks])]
                           ).then_inc(up_ready, 1)

            def down(e, i, last=False):
                half, c, f, slot = i // (CH * FT) % HALVES, i // FT % CH, i % FT, i % HS
                _, _, down_hi = half_weights(w_hi, half)
                _, _, down_lo = half_weights(w_lo, half)
                pe.wait_ge(hid_lo_done, STEPS * e + i + 1)
                if f == 0:
                    at_least(pe, part_done, 2 * CH * e + i // FT - 1)
                    if last and i // FT > CH:
                        pe.wait_ge(y_done, c)
                for d in range(DK):
                    cols = slice(d * P, (d + 1) * P)
                    ins = accumulate(ps_d[c % 2][:, d, :],
                                     three(down_hi[:, f, cols], down_lo[:, f, cols], hs[:, 0, slot, :], hs[:, 1, slot, :]),
                                     first=f == 0, last=f == FT - 1)
                if f == FT - 1:
                    ins.then_inc(down_ready, 1)

            def down_rows(tiles):
                _, _, down_hi = half_weights(w_hi, HALVES - 1)
                _, _, down_lo = half_weights(w_lo, HALVES - 1)
                pe.wait_ge(hid_lo_done, STEPS * E - FT + tiles[-1] + 1)
                if tiles[0] == 0:
                    pe.wait_ge(part_done, 2 * CH * E - 2)
                    pe.wait_ge(y_done, CH - 1)
                for j in range(BC // 2):
                    for f in tiles:
                        slot = (STEPS - FT + f) % HS
                        for i in range(2):
                            toks = slice((2 * j + i) * TQ, (2 * j + i + 1) * TQ)
                            ins = accumulate(ps_y[1][:, j, i * D:(i + 1) * D],
                                             three(hs[:, 0, slot, toks], hs[:, 1, slot, toks], down_hi[:, f, :], down_lo[:, f, :]),
                                             first=f == 0 and i == 0, last=f == FT - 1 and i == 1)
                    if tiles[-1] == FT - 1:
                        ins.then_inc(end_ready, 1)

            def sum_rows(n):
                c = (n - 1) % CH
                pe.wait_ge(acc_done, 2 * CH * E - 2 * CH + n)
                for j in range(BC):
                    b, bank, at = c * BC + j, j * D // 512, j * D % 512
                    for d in range(DK):
                        ins = nc.tensor.transpose(ps_y[c % 2][:, bank, at + d * P:at + (d + 1) * P], acc[:, d, b * TQ:(b + 1) * TQ], ident[:])
                ins.then_inc(y_ready, 1)

            def expert(e, first=False, last=False):
                for s in range(EARLY if first else 0, STEPS):
                    gate_up(e, s, first)
                    if last and s - LAG >= STEPS - FT:
                        down_rows([s - LAG - STEPS + FT])
                    else:
                        down(e, s - LAG, last)
                    if last and s > STEPS // 2 and s % FT == 0:
                        sum_rows((s - STEPS // 2) // FT - 1)
                if last:
                    sum_rows(CH - 1)
                    down_rows(range(FT - LAG, FT))

            pair(0, 0)
            pair(1, 1)
            with pe.Fori(1, PAIRS // 2 - 1) as n:
                pair(2 * n, 0)
                pair(2 * n + 1, 1)
            for p in range(PAIRS - 2, PAIRS):
                pair(p, p % 2)
            last_pair = PAIRS - 1
            transpose_probs(last_pair, 0)
            gate_up(0, 2)
            transpose_probs(last_pair, 1)
            pe.wait_ge(probs_done, 2 * PAIRS)
            pe.wait_ge(pt_lo_done, 2 * PAIRS - 1)
            down(0, 0)
            mix_ctx(last_pair)
            down(0, 1)
            transpose_mix(last_pair)
            gate_up(0, 3)
            values(last_pair)
            transpose_norm2(last_pair - 1)
            gate_up(0, 4, first=True)
            down(0, 2)
            down(0, 3)
            route(last_pair - 1)
            transpose_norm2(last_pair)
            gate_up(0, 5)
            route(last_pair)
            gate_up(0, 6)
            gate_up(0, 7)
            pe.wait_ge(logits_done, PAIRS)
            down(0, 4)
            pe.wait_ge(cw_ready, 1)
            pe.wait_ge(act_done, EARLY - 1)
            nc.tensor.transpose(ps_cw, cw_t[:, :, :].rearrange("p e b -> p (e b)"), ident[0:TQ, 0:TQ]).then_inc(cw_rows_ready, 1)
            down(0, 5)

            expert(0, first=True)
            with pe.Fori(1, E - 1) as e:
                expert(e)
            expert(E - 1, last=True)


_INS = ['x', 'ctx_1024', 'L0_xattn_Wq', 'L0_xattn_bq', 'L0_xattn_Wk', 'L0_xattn_bk', 'L0_xattn_Wv', 'L0_xattn_bv',
        'L0_ffn_w_router', 'L0_ffn_w_gating', 'L0_ffn_w_gate', 'L0_ffn_w_up', 'L0_ffn_w_down']


def kernel(**inputs):
    import numpy as _np
    import concourse.bacc as _bacc
    from concourse import mybir as _mybir
    from concourse.bass_utils import run_bass_kernel_spmd as _run

    nc = _bacc.Bacc("TRN2", target_bir_lowering=False, num_devices=1)
    arrays, args = {}, []
    for name in _INS:
        a = _np.ascontiguousarray(inputs[name])
        arrays[f"in_{name}"] = a
        args.append(nc.dram_tensor(f"in_{name}", a.shape, _mybir.dt.from_np(a.dtype), kind="ExternalInput").ap())
    shape = tuple(inputs['x'].shape)
    args.append(nc.dram_tensor("out_dram", shape, _mybir.dt.from_np(_np.dtype('float32')), kind="ExternalOutput").ap())
    xattn_ffn_kernel(nc, *args)
    return _run(nc, [arrays], core_ids=[0]).results[0]["out_dram"]
```
